# Optimizing a Trainium2 kernel written in Bass

```python
import numpy as np
import jax
import jax.numpy as jnp

def _softmax(x, axis=-1):
    return jax.nn.softmax(x, axis=axis)

def _gelu(x):
    return jax.nn.gelu(x, approximate=True)

def _silu(x):
    return jax.nn.silu(x)

def _sigmoid(x):
    return jax.nn.sigmoid(x)

def _layernorm(x, axis=-1, eps=1e-05):
    m = jnp.mean(x, axis=axis, keepdims=True)
    v = jnp.var(x, axis=axis, keepdims=True)
    return (x - m) / jnp.sqrt(v + eps)

def _scatter_add(tgt, idx, src, axis=0):
    return tgt.at[idx].add(src)

def _segment_sum(src, seg, n):
    return jax.ops.segment_sum(src, seg, n)
kernel_name = 'mk_xattn_ffn_d1_seqx_r4_1bff6b'

def setup_inputs(seed: int=0):
    np.random.seed(seed)
    _w = jnp.asarray

    def _rec_inputs():
        import jax
        import jax.numpy as jnp
        _rk = jax.random.key(seed)
        x = -0.0003929 + 0.9999 * jax.random.normal(jax.random.fold_in(_rk, 1), (4, 512, 512), jnp.float32)
        _lenS = 512 - jax.random.randint(jax.random.fold_in(_rk, 7), (4,), 0, max(1, 512 // 4) + 1, jnp.int32)
        _lenS2 = 512 - jax.random.randint(jax.random.fold_in(_rk, 8), (4,), 0, max(1, 512 // 4) + 1, jnp.int32)
        _ctx_2048P = jax.random.normal(jax.random.fold_in(_rk, 11), (4, 16, 512), jnp.float32)
        _ctx_2048c = jax.random.dirichlet(jax.random.fold_in(_rk, 511), 0.3 * jnp.ones((16,), jnp.float32), (4, 512))
        _ctx_2048t = jnp.einsum('bsk,bkd->bsd', _ctx_2048c, _ctx_2048P)
        _ctx_2048t = _ctx_2048t * jax.lax.rsqrt(jnp.mean(jnp.square(_ctx_2048t)) + 1e-12) * 0.953939
        ctx_2048 = -0.000514642 + 1.00011 * (_ctx_2048t + 0.3 * jax.random.normal(jax.random.fold_in(_rk, 611), (4, 512, 512), jnp.float32))
        return (x, ctx_2048)
    x, ctx_2048 = _rec_inputs()

    def _L0_xattn_setup():
        import jax, jax.numpy as jnp
        import numpy as np
        DIM = 512
        NHEADS = 32
        HEAD_DIM = DIM // NHEADS
        EPS = 1e-06

        def _rmsnorm(t):
            return t * jax.lax.rsqrt(jnp.mean(t * t, axis=-1, keepdims=True) + EPS)
        key = jax.random.key(seed)
        kx, kc, kq, kk, kv = jax.random.split(key, 5)
        x = jax.random.normal(kx, (2, 1024, DIM), dtype=jnp.float32)
        context = jax.random.normal(kc, (2, 128, DIM), dtype=jnp.float32)
        std = 0.02
        Wq = jax.random.normal(kq, (DIM, DIM), dtype=jnp.float32) * std
        Wk = jax.random.normal(kk, (DIM, DIM), dtype=jnp.float32) * std
        Wv = jax.random.normal(kv, (DIM, DIM), dtype=jnp.float32) * std
        return {'x': x, 'context': context, 'Wq': Wq, 'Wk': Wk, 'Wv': Wv}
    _L0_xattn_all = _L0_xattn_setup()
    _L0_xattn_in = {k: v for k, v in _L0_xattn_all.items() if k in ('Wq', 'Wk', 'Wv')}
    del _L0_xattn_all

    def _L0_ffn_setup():
        import jax, jax.numpy as jnp
        import numpy as np
        H = 512
        I = 512
        E_ROUTED = 7
        NS = 1
        TOPK = 2
        TEMP = 1.0

        def _moe_forward(x, Wr, br, gate_bias, Wup, bup, Wgate, bgate, Wdown, bdown, Wsu, bsu, Wsg, bsg, Wsd, bsd):
            B, S, _ = x.shape
            xt = x.reshape(-1, H)
            N = xt.shape[0]
            gate = (xt @ Wr + br) / TEMP
            bias_gate = gate + gate_bias
            _, ids = jax.lax.top_k(bias_gate, TOPK)
            sel_logits = jnp.take_along_axis(gate, ids, axis=-1)
            masked = jnp.full_like(gate, -jnp.inf)
            masked = masked.at[jnp.arange(N)[:, None], ids].set(sel_logits)
            probs = jax.nn.softmax(masked, axis=-1)
            u = jnp.einsum('nh,ehi->eni', xt, Wup) + bup[:, None, :]
            g = jax.nn.silu(jnp.einsum('eni,eij->enj', u, Wgate) + bgate[:, None, :]) * u
            eo = jnp.einsum('enj,ejh->enh', g, Wdown) + bdown[:, None, :]
            out = jnp.einsum('ne,enh->nh', probs, eo)
            su = (xt @ Wsu + bsu).reshape(N, NS, I)
            sg = jax.nn.silu(su @ Wsg + bsg) * su
            so = (sg @ Wsd + bsd).sum(axis=1)
            out = out + so
            return out.reshape(B, S, H)
        key = jax.random.key(seed)
        ks = jax.random.split(key, 20)
        s = lambda fan_in: 1.0 / np.sqrt(fan_in)
        inp = {'x': jax.random.normal(ks[0], (4, 256, H), dtype=jnp.float32), 'Wr': jax.random.normal(ks[1], (H, E_ROUTED), jnp.float32) * s(H), 'br': jax.random.normal(ks[2], (E_ROUTED,), jnp.float32) * s(H), 'gate_bias': jnp.zeros((E_ROUTED,), jnp.float32), 'Wup': jax.random.normal(ks[3], (E_ROUTED, H, I), jnp.float32) * s(H), 'bup': jax.random.normal(ks[4], (E_ROUTED, I), jnp.float32) * s(H), 'Wgate': jax.random.normal(ks[5], (E_ROUTED, I, I), jnp.float32) * s(I), 'bgate': jax.random.normal(ks[6], (E_ROUTED, I), jnp.float32) * s(I), 'Wdown': jax.random.normal(ks[7], (E_ROUTED, I, H), jnp.float32) * s(I), 'bdown': jax.random.normal(ks[8], (E_ROUTED, H), jnp.float32) * s(I), 'Wsu': jax.random.normal(ks[9], (H, NS * I), jnp.float32) * s(H), 'bsu': jax.random.normal(ks[10], (NS * I,), jnp.float32) * s(H), 'Wsg': jax.random.normal(ks[11], (I, I), jnp.float32) * s(I), 'bsg': jax.random.normal(ks[12], (I,), jnp.float32) * s(I), 'Wsd': jax.random.normal(ks[13], (I, H), jnp.float32) * s(I), 'bsd': jax.random.normal(ks[14], (H,), jnp.float32) * s(I)}
        return inp
    _L0_ffn_all = _L0_ffn_setup()
    _L0_ffn_in = {k: v for k, v in _L0_ffn_all.items() if k in ('Wr', 'br', 'gate_bias', 'Wup', 'bup', 'Wgate', 'bgate', 'Wdown', 'bdown', 'Wsu', 'bsu', 'Wsg', 'bsg', 'Wsd', 'bsd')}
    del _L0_ffn_all
    return {'x': x, 'ctx_2048': ctx_2048, 'L0_xattn_Wq': _L0_xattn_in['Wq'], 'L0_xattn_Wk': _L0_xattn_in['Wk'], 'L0_xattn_Wv': _L0_xattn_in['Wv'], 'L0_ffn_Wr': _L0_ffn_in['Wr'], 'L0_ffn_br': _L0_ffn_in['br'], 'L0_ffn_gate_bias': _L0_ffn_in['gate_bias'], 'L0_ffn_Wup': _L0_ffn_in['Wup'], 'L0_ffn_bup': _L0_ffn_in['bup'], 'L0_ffn_Wgate': _L0_ffn_in['Wgate'], 'L0_ffn_bgate': _L0_ffn_in['bgate'], 'L0_ffn_Wdown': _L0_ffn_in['Wdown'], 'L0_ffn_bdown': _L0_ffn_in['bdown'], 'L0_ffn_Wsu': _L0_ffn_in['Wsu'], 'L0_ffn_bsu': _L0_ffn_in['bsu'], 'L0_ffn_Wsg': _L0_ffn_in['Wsg'], 'L0_ffn_bsg': _L0_ffn_in['bsg'], 'L0_ffn_Wsd': _L0_ffn_in['Wsd'], 'L0_ffn_bsd': _L0_ffn_in['bsd']}

def reference(x, ctx_2048, L0_xattn_Wq, L0_xattn_Wk, L0_xattn_Wv, L0_ffn_Wr, L0_ffn_br, L0_ffn_gate_bias, L0_ffn_Wup, L0_ffn_bup, L0_ffn_Wgate, L0_ffn_bgate, L0_ffn_Wdown, L0_ffn_bdown, L0_ffn_Wsu, L0_ffn_bsu, L0_ffn_Wsg, L0_ffn_bsg, L0_ffn_Wsd, L0_ffn_bsd):
    import jax
    import jax.numpy as jnp

    def _L0_xattn_ref(x, context, Wq, Wk, Wv):
        import jax, jax.numpy as jnp
        import numpy as np
        DIM = 512
        NHEADS = 32
        HEAD_DIM = DIM // NHEADS
        EPS = 1e-06

        def _rmsnorm(t):
            return t * jax.lax.rsqrt(jnp.mean(t * t, axis=-1, keepdims=True) + EPS)
        b, n, _ = x.shape
        m = context.shape[1]
        q = x @ Wq.T
        k_raw = context @ Wk.T
        v_raw = context @ Wv.T
        q = q.reshape(b, n, NHEADS, HEAD_DIM).transpose(0, 2, 1, 3)
        kv = jnp.concatenate([k_raw, v_raw], axis=-1)
        kv = kv.reshape(b, m, NHEADS, HEAD_DIM, 2)
        k = kv[..., 0].transpose(0, 2, 1, 3)
        v = kv[..., 1].transpose(0, 2, 1, 3)
        q = _rmsnorm(q)
        k = _rmsnorm(k)
        scale = HEAD_DIM ** (-0.5)
        scores = jnp.einsum('bhnd,bhmd->bhnm', q, k) * scale
        attn = jax.nn.softmax(scores, axis=-1)
        out = jnp.einsum('bhnm,bhmd->bhnd', attn, v)
        return out.transpose(0, 2, 1, 3).reshape(b, n, NHEADS * HEAD_DIM)

    def _L0_ffn_ref(x, Wr, br, gate_bias, Wup, bup, Wgate, bgate, Wdown, bdown, Wsu, bsu, Wsg, bsg, Wsd, bsd):
        import jax, jax.numpy as jnp
        import numpy as np
        H = 512
        I = 512
        E_ROUTED = 7
        NS = 1
        TOPK = 2
        TEMP = 1.0

        def _moe_forward(x, Wr, br, gate_bias, Wup, bup, Wgate, bgate, Wdown, bdown, Wsu, bsu, Wsg, bsg, Wsd, bsd):
            B, S, _ = x.shape
            xt = x.reshape(-1, H)
            N = xt.shape[0]
            gate = (xt @ Wr + br) / TEMP
            bias_gate = gate + gate_bias
            _, ids = jax.lax.top_k(bias_gate, TOPK)
            sel_logits = jnp.take_along_axis(gate, ids, axis=-1)
            masked = jnp.full_like(gate, -jnp.inf)
            masked = masked.at[jnp.arange(N)[:, None], ids].set(sel_logits)
            probs = jax.nn.softmax(masked, axis=-1)
            u = jnp.einsum('nh,ehi->eni', xt, Wup) + bup[:, None, :]
            g = jax.nn.silu(jnp.einsum('eni,eij->enj', u, Wgate) + bgate[:, None, :]) * u
            eo = jnp.einsum('enj,ejh->enh', g, Wdown) + bdown[:, None, :]
            out = jnp.einsum('ne,enh->nh', probs, eo)
            su = (xt @ Wsu + bsu).reshape(N, NS, I)
            sg = jax.nn.silu(su @ Wsg + bsg) * su
            so = (sg @ Wsd + bsd).sum(axis=1)
            out = out + so
            return out.reshape(B, S, H)
        return _moe_forward(x, Wr, br, gate_bias, Wup, bup, Wgate, bgate, Wdown, bdown, Wsu, bsu, Wsg, bsg, Wsd, bsd)
    x = x + _L0_xattn_ref(_layernorm(x, axis=-1), ctx_2048, L0_xattn_Wq, L0_xattn_Wk, L0_xattn_Wv)
    x = x + _L0_ffn_ref(_layernorm(x, axis=-1), L0_ffn_Wr, L0_ffn_br, L0_ffn_gate_bias, L0_ffn_Wup, L0_ffn_bup, L0_ffn_Wgate, L0_ffn_bgate, L0_ffn_Wdown, L0_ffn_bdown, L0_ffn_Wsu, L0_ffn_bsu, L0_ffn_Wsg, L0_ffn_bsg, L0_ffn_Wsd, L0_ffn_bsd)
    return x

_drawn_inputs = setup_inputs


def setup_inputs(seed=0):
    import zlib

    import numpy as np

    out = dict(_drawn_inputs(seed))
    spreads = {'L0_ffn_gate_bias': (0.0, 0.1)}
    factors = {'L0_ffn_bgate': 3.566, 'L0_ffn_bsg': 2.676}
    for name, (base, spread) in spreads.items():
        noise = np.random.default_rng([zlib.crc32(name.encode()), seed]).standard_normal(out[name].shape)
        drawn = base * np.exp(spread * noise) if base else spread * noise
        out[name] = jnp.asarray(drawn.astype(out[name].dtype))
    for name, factor in factors.items():
        out[name] = (out[name] * factor).astype(out[name].dtype)
    return out
```

```python
from contextlib import ExitStack

import concourse.bass as bass
from concourse import mybir

FP32 = mybir.dt.float32
FP32R = mybir.dt.float32r
ALU = mybir.AluOpType
ACT = mybir.ActivationFunctionType
AX = mybir.AxisListType

P = 128


class Tally:

    def __init__(self, sem):
        self.sem, self.const, self.turns = sem, 0, 0

    def next(self, by=1):
        self.const += by
        return self.now()

    def now(self, less=0):
        return self.turns + (self.const - less)

    def past(self, n):
        return not isinstance(self.turns, int) or self.const > n


def moe_layer(nc, x, ctx_t, wq_t, wkv_t, w_all, b_up_gate, b_down, w_router, b_router, gate_bias, out):
    TOKENS, D = x.shape
    BATCH = ctx_t.shape[0]
    SEQ = TOKENS // BATCH
    CTX = ctx_t.shape[2]
    DC = D // P
    HD = 16
    TILES = TOKENS // P
    BT = SEQ // P
    MT = CTX // P
    GROUPS = DC
    GH = P // HD
    PAIRS = GH // 2
    E = w_all.shape[0]
    ER = E - 1
    LN_EPS, RMS_EPS = 1e-5, 1e-6

    with ExitStack() as ctx:
        att = ExitStack()
        def sb(name, shape, dt=FP32):
            return ctx.enter_context(nc.sbuf_tensor(name, shape, dt))

        def ps(name, shape):
            return att.enter_context(nc.psum_tensor(name, shape, FP32))

        def sem(name):
            return ctx.enter_context(nc.semaphore(name))

        x_sb = sb("x_sb", [P, TILES, D])
        ident = sb("ident", [P, P])
        stats = sb("stats", [P, 6])
        mv = sb("mv", [P, TILES, 2])
        rstd = sb("rstd", [P, TILES])
        power = sb("power", [P, 2 * 8])
        mean_sq = sb("mean_sq", [P, 2 * 8])
        rsqrt = sb("rsqrt", [P, 2 * 8])

        def asb(name, shape, dt=FP32):
            return att.enter_context(nc.sbuf_tensor(name, shape, dt))

        wq = asb("wq", [P, DC, D])
        wkv = asb("wkv", [P, DC, GROUPS, 2 * P])
        ctx_sb = asb("ctx_sb", [P, DC, CTX])
        xn_t = asb("xn_t", [P, DC, SEQ])
        xn = asb("xn", [P, 2, D])
        raw = asb("raw", [P, 2 * GH, HD])
        sq = asb("sq", [P, 2 * GH, HD])
        qn = asb("qn", [P, 2 * GH, HD])
        split = asb("split", [P, 2, 2, GH, 4, HD])
        q_stack = asb("q_stack", [P, 2, PAIRS, SEQ], FP32R)
        k_stack = asb("k_stack", [P, 2, PAIRS, CTX], FP32R)
        v_sb = asb("v_sb", [P, 2, MT, GH, 2 * HD])
        probs = asb("probs", [P, 2, 4, SEQ])
        o_sb = asb("o_sb", [P, SEQ])
        o_n = asb("o_n", [P, BT, 4, HD])
        rec = asb("rec", [P, BT, 4])

        scores = ps("scores", [P, 2, 2, SEQ])
        o_ps = ps("o_ps", [P, SEQ])
        pj = ps("pj", [P, 512])
        tr = ps("tr", [P, 2, 512])

        w_loaded = sem("w_loaded")
        x_first = sem("x_first")
        x_rest = sem("x_rest")
        ctx_loaded = sem("ctx_loaded")
        ones_set = sem("ones_set")
        ident_zero = sem("ident_zero")
        ident_set = sem("ident_set")
        xn_ready = sem("xn_ready")
        tr_ready = sem("tr_ready")
        tr_free = sem("tr_free")
        pj_ready = sem("pj_ready")
        pj_free = sem("pj_free")
        split_ready = sem("split_ready")
        sc_ready = sem("sc_ready")
        p_ready = sem("p_ready")
        pv_done = sem("pv_done")
        o_ready = sem("o_ready")
        o_evac = sem("o_evac")
        dve_step = sem("dve_step")
        mean_ready = sem("mean_ready")
        power_set = sem("power_set")
        rsqrt_ready = sem("rsqrt_ready")

        block = att.enter_context(nc.Block())

        def loop_over_batches(engine, tallies, turn):
            with engine.Fori(1, BATCH) as r:
                before = [t.const for t in tallies]
                per_turn = [TURN[t.sem.name] for t in tallies]
                for t, n in zip(tallies, per_turn):
                    t.turns = (r - 1) * n
                turn(r)
            for t, n, was in zip(tallies, per_turn, before):
                assert t.const - was == n, (t.sem.name, t.const - was)
                t.turns = 0
                t.const += n * (BATCH - 2)

        TURN = {"xn_ready": BT, "tr_ready": BT + 4 * (2 * BT + 2), "tr_free": BT + 4 * (2 * BT + 2),
                "pj_ready": 4 * BT, "pj_free": 4 * BT, "split_ready": 4 * BT, "sc_ready": 4 * 16,
                "p_ready": 4 * 16, "pv_done": 4 * 8, "o_ready": 8, "o_evac": 8,
                "dve_step": 8 * 1 + 16 * 5,
                "rsqrt_ready": 4 * BT}

        @block.gpsimd
        def _(pool):
            nc.gpsimd.memset(ident[:], 0.0).then_inc(ident_zero, 1)
            nc.gpsimd.memset(v_sb[:, :, :, :, HD:], 1.0).then_inc(ones_set, 1)
            pool.wait_ge(ident_zero, 1)
            nc.gpsimd.affine_select(out=ident[:], in_=ident[:], compare_op=ALU.not_equal, fill=1.0, base=0,
                                    pattern=[[-1, P]], channel_multiplier=1).then_inc(ident_set, 1)
            nc.gpsimd.memset(power[:], -0.5).then_inc(power_set, 1)
            pool.wait_ge(power_set, 1)
            with pool.Fori(0, 2 + TILES * GROUPS) as i:
                pool.wait_ge(mean_ready, i + 1)
                nc.gpsimd.tensor_tensor(rsqrt[:], mean_sq[:], power[:], ALU.pow).then_inc(rsqrt_ready, 1)

        @block.sync
        def _(sp):
            x_v = x.rearrange("(t p) d -> p t d", p=P)
            sp.dma_start(x_sb[:, 0:BT, :], x_v[:, 0:BT, :]).then_inc(x_first, 16)
            sp.dma_start(wq[:], wq_t.rearrange("(c p) n -> p c n", p=P)).then_inc(w_loaded, 16)
            sp.dma_start(ctx_sb[:], ctx_t[0, :, :].rearrange("(c p) m -> p c m", p=P)).then_inc(ctx_loaded, 16)
            sp.dma_start(wkv[:], wkv_t.rearrange("(c p) (g n) -> p c g n", p=P, n=2 * P)).then_inc(w_loaded, 16)
            sp.dma_start(x_sb[:, BT:, :], x_v[:, BT:, :]).then_inc(x_rest, 16)
            with sp.Fori(1, BATCH) as b:
                sp.wait_ge(pj_ready, b * (GROUPS * BT))
                sp.dma_start(ctx_sb[:], ctx_t[bass.ds(b, 1), :, :].rearrange("a (c p) m -> p (a c) m", p=P))\
                  .then_inc(ctx_loaded, 16)

        @block.tensor
        def _(pe):
            xn_r, trr, trf = Tally(xn_ready), Tally(tr_ready), Tally(tr_free)
            pjr, spl = Tally(pj_ready), Tally(split_ready)
            scr, pvd, orr = Tally(sc_ready), Tally(pv_done), Tally(o_ready)
            tallies = [xn_r, trr, pjr, spl, scr, pvd, orr]

            def transposes(sources):
                trr.next()
                if trr.past(2):
                    pe.wait_ge(tr_free, trr.now(2))
                for i, src in enumerate(sources):
                    last = nc.tensor.transpose(tr[:, trr.const % 2, i * P:(i + 1) * P], src, ident[:])
                last.then_inc(tr_ready, 1)

            def norm_transposes(t):
                pe.wait_ge(xn_ready, xn_r.next())
                transposes([xn[:, t % 2, c * P:(c + 1) * P] for c in range(DC)])

            def project(g, t, batch):
                if batch is not None:
                    pe.wait_ge(ctx_loaded, batch * 16 + 16)
                    pe.wait_ge(tr_free, trr.now())
                pjr.next()
                if pjr.past(1):
                    pe.wait_ge(pj_free, pjr.now(1))
                for c in range(DC):
                    nc.tensor.matmul(pj[:, 0:P], xn_t[:, c, t * P:(t + 1) * P], wq[:, c, g * P:(g + 1) * P],
                                     start=(c == 0), stop=(c == DC - 1))
                for c in range(DC):
                    last = nc.tensor.matmul(pj[:, P:3 * P], ctx_sb[:, c, t * P:(t + 1) * P], wkv[:, c, g, :],
                                            start=(c == 0), stop=(c == DC - 1))
                last.then_inc(pj_ready, 1)

            def stack_transposes(t):
                pe.wait_ge(split_ready, spl.next())
                for qk in range(2):
                    rows = split[:, t % 2, qk].rearrange("p h s d -> p (h s d)")
                    transposes([rows[:, i * P:(i + 1) * P] for i in range(PAIRS)])

            def score(par, s):
                g4, mt = divmod(s, MT)
                for a in range(2):
                    scr.next()
                    if scr.past(2):
                        pe.wait_ge(p_ready, scr.now(2))
                    hp = g4 * 2 + a
                    for i in range(2):
                        rows = slice(64 * i, 64 * i + 64)
                        last = nc.tensor.matmul(scores[:, a, i, :], k_stack[rows, par, hp, mt * P:(mt + 1) * P],
                                                q_stack[rows, par, hp, :], start=True, stop=True)
                    last.then_inc(sc_ready, 1)

            def weigh(par, s, behind):
                g4, mt = divmod(s, MT)
                pe.wait_ge(p_ready, scr.now(behind))
                if mt == 0:
                    if orr.past(0):
                        pe.wait_ge(o_evac, orr.now())
                for j in range(4):
                    last = nc.tensor.matmul(o_ps[32 * j:32 * j + 32, :], v_sb[:, par, mt, 4 * g4 + j, :],
                                            probs[:, s % 2, j, :], start=(mt == 0), stop=(mt == MT - 1))
                pvd.next()
                last.then_inc(pv_done, 1)
                if mt == MT - 1:
                    orr.next()

            def out_transposes():
                pe.wait_ge(o_evac, orr.now())
                transposes([o_sb[:, t * P:(t + 1) * P] for t in range(BT)])

            def unit(k, batch, first=False, last=False):
                par, nxt = k % 2, (k + 1) % GROUPS
                for s in range(8):
                    if s == 0:
                        pe.wait_ge(tr_free, trr.now())
                    score(par, s)
                    if k == GROUPS - 1 and s % 2 == 0 and not last:
                        norm_transposes(s // 2)
                    if s:
                        weigh(par, s - 1, 2)
                    elif not first:
                        weigh(1 - par, 7, 2)
                    if not last and s % 2 == 0:
                        project(nxt, s // 2, batch + 1 if k == GROUPS - 1 else None)
                    if s == 5 or (s == 1 and not first):
                        out_transposes()
                    if not last and s % 2:
                        stack_transposes(s // 2)

            pe.wait_ge(ident_set, 1)
            pe.wait_ge(ones_set, 1)
            pe.wait_ge(w_loaded, 32)
            for t in range(BT):
                norm_transposes(t)
                project(0, t, 0)
                stack_transposes(t)
            unit(0, 0, first=True)
            unit(1, 0)
            unit(2, 0)

            def turn(r):
                unit(3, r - 1)
                for k in range(3):
                    unit(k, r)
            loop_over_batches(pe, tallies, turn)
            unit(3, BATCH - 1, last=True)
            weigh(1, 7, 0)
            out_transposes()

        @block.scalar
        def _(act):
            scr, steps = Tally(sc_ready), Tally(pv_done)

            def unit():
                for s in range(8):
                    for a in range(2):
                        act.wait_ge(sc_ready, scr.next())
                        if a == 0 and steps.past(1):
                            act.wait_ge(pv_done, steps.now(1))
                        nc.scalar.activation(probs[:, s % 2, 2 * a:2 * a + 2, :], scores[:, a], ACT.Exp,
                                             scale=float(HD) ** 0.5).then_inc(p_ready, 1)
                    steps.next()

            for _ in range(3):
                unit()

            def turn(r):
                for _ in range(4):
                    unit()
            loop_over_batches(act, [scr, steps], turn)
            unit()

        @block.vector
        def _(dve):
            trr, pjr, orr, step = Tally(tr_ready), Tally(pj_ready), Tally(o_ready), Tally(dve_step)
            rsq = Tally(rsqrt_ready)
            tallies = [trr, pjr, orr, step, rsq]

            def done(ins):
                ins.then_inc(dve_step, 1)
                dve.wait_ge(dve_step, step.next())

            def root():
                dve.wait_ge(rsqrt_ready, rsq.next())

            def stat(t):
                done(nc.vector.bn_stats(stats[:], x_sb[:, t, :]))
                done(nc.vector.bn_aggr(mv[:, t, :], stats[:]))

            def deviations(tiles):
                nc.vector.tensor_scalar(mean_sq[:, tiles], mv[:, tiles, 1], LN_EPS, None, ALU.add)\
                  .then_inc(mean_ready, 1)
                root()
                done(nc.vector.tensor_copy(rstd[:, tiles], rsqrt[:, tiles]))

            def norm(batch, t):
                tile = batch * BT + t
                nc.vector.tensor_scalar(xn[:, t % 2, :], x_sb[:, tile, :], mv[:, tile, 0:1], rstd[:, tile:tile + 1]
                                        if isinstance(tile, int) else rstd[:, bass.ds(tile, 1)],
                                        ALU.subtract, ALU.mult).then_inc(xn_ready, 1)

            def evacuate(dst):
                dve.wait_ge(tr_ready, trr.next())
                src = tr[:, trr.const % 2, :].rearrange("p (a b) -> p a b", b=P)
                nc.vector.tensor_copy(dst, src).then_inc(tr_free, 1)

            def norm_out(t):
                evacuate(xn_t[:, :, t * P:(t + 1) * P])

            def project_out(par, t):
                dve.wait_ge(pj_ready, pjr.next())
                done(nc.vector.tensor_copy(raw[:], pj[:, 0:2 * P].rearrange("p (h d) -> p h d", d=HD)))
                done(nc.vector.tensor_tensor(sq[:], raw[:], raw[:], ALU.mult))
                done(nc.vector.tensor_reduce(mean_sq[:], sq[:], axis=AX.X, op=ALU.add))
                nc.vector.tensor_scalar(mean_sq[:], mean_sq[:], HD * RMS_EPS, None, ALU.add).then_inc(mean_ready, 1)
                nc.vector.tensor_copy(v_sb[:, par, t, :, 0:HD], pj[:, 2 * P:3 * P].rearrange(
                    "p (h d) -> p h d", d=HD)).then_inc(pj_free, 1)
                root()
                done(nc.vector.tensor_tensor(qn[:], raw[:], rsqrt[:].unsqueeze(2).to_broadcast([P, 2 * GH, HD]),
                                             ALU.mult))
                q, k = split[:, t % 2, 0], split[:, t % 2, 1]
                twice = [P, GH, 2, HD]
                q_in = qn[:, 0:GH, :].unsqueeze(2).to_broadcast(twice)
                k_in = qn[:, GH:, :].unsqueeze(2).to_broadcast(twice)
                nc.vector.tensor_copy(q[:, :, 0:2, :].bitcast(FP32R), q_in)
                done(nc.vector.tensor_copy(k[:, :, 0:4:2, :].bitcast(FP32R), k_in))
                nc.vector.tensor_tensor(q[:, :, 2:4, :].bitcast(FP32R), q_in, q[:, :, 0:2, :], ALU.subtract)
                nc.vector.tensor_tensor(k[:, :, 1:4:2, :].bitcast(FP32R), k_in, k[:, :, 0:4:2, :], ALU.subtract)\
                  .then_inc(split_ready, 1)

            def stacks_out(par, t):
                evacuate(q_stack[:, par, :, t * P:(t + 1) * P])
                evacuate(k_stack[:, par, :, t * P:(t + 1) * P])

            def group_out():
                dve.wait_ge(pv_done, orr.next() * MT)
                nc.vector.tensor_copy(o_sb[:], o_ps[:]).then_inc(o_evac, 1)

            def finalize(batch, g, g4):
                dve.wait_ge(tr_ready, trr.next())
                o_t = tr[:, trr.const % 2, :].rearrange("p (t h d) -> p t h d", t=BT, d=2 * HD)
                done(nc.vector.reciprocal(rec[:], o_t[:, :, :, HD]))
                nc.vector.tensor_tensor(o_n[:], o_t[:, :, :, 0:HD],
                                        rec[:].unsqueeze(3).to_broadcast([P, BT, 4, HD]), ALU.mult)\
                  .then_inc(tr_free, 1)
                dve.wait_ge(tr_free, trr.now())
                cols = g * P + g4 * 4 * HD
                xs = x_sb[:, bass.ds(batch * BT, BT), cols:cols + 4 * HD]
                nc.vector.tensor_tensor(xs, xs, o_n[:].rearrange("p t h d -> p t (h d)"), ALU.add)

            def unit(k, batch, first=False, last=False, between=None):
                par = k % 2
                before = (batch, k - 1) if k else (batch - 1, GROUPS - 1)
                for s in range(8):
                    if k == GROUPS - 1 and s == 0 and not last:
                        norm(batch + 1, 0)
                        norm(batch + 1, 1)
                    if k == GROUPS - 1 and s % 2 == 0 and not last:
                        norm_out(s // 2)
                        if s // 2 + 2 < BT:
                            norm(batch + 1, s // 2 + 2)
                    if s == 4 or (s == 0 and not first):
                        group_out()
                    if not last and s % 2 == 0:
                        project_out(1 - par, s // 2)
                    if s == 1 and not first:
                        finalize(*before, 1)
                    if s == 5:
                        finalize(batch, k, 0)
                    if not last and s % 2:
                        stacks_out(1 - par, s // 2)
                    if between:
                        between(s)

            nc.vector.memset(mean_sq[:], 1.0)
            dve.wait_ge(x_first, 16)
            for t in range(BT):
                stat(t)
            deviations(slice(0, BT))
            norm(0, 0)
            norm(0, 1)
            for t in range(BT):
                norm_out(t)
                if t + 2 < BT:
                    norm(0, t + 2)
                project_out(0, t)
                stacks_out(0, t)
            unit(0, 0, first=True)
            dve.wait_ge(x_rest, 16)
            unit(1, 0, between=lambda s: stat(BT + s))
            unit(2, 0, between=lambda s: stat(BT + 8 + s) if s < TILES - BT - 8 else None)
            deviations(slice(BT, TILES))

            def turn(r):
                unit(3, r - 1)
                for k in range(3):
                    unit(k, r)
            loop_over_batches(dve, tallies, turn)
            unit(3, BATCH - 1, last=True)
            group_out()
            finalize(BATCH - 1, GROUPS - 1, 1)

        att.close()

        TG = 512
        GT = TG // P
        NG = TOKENS // TG
        xt = sb("xt", [P, DC, TOKENS])
        x2 = sb("x2", [P, 2, D])
        wr = sb("wr", [P, DC, ER])
        brt = sb("brt", [P, ER])
        gbt = sb("gbt", [P, ER])
        gate = sb("gate", [P, TILES, ER])
        biased = sb("biased", [P, TILES, ER])
        key = sb("key", [P, TILES, ER])
        hot = sb("hot", [P, 2, TILES, ER])
        order = sb("order", [P, ER])
        top = sb("top", [P, TILES])
        lg = sb("lg", [P, 2, TILES])
        probs_e = sb("probs_e", [P, TILES, E])
        w_sb = sb("w_sb", [P, 2, 3, DC, D])
        b_ug = sb("b_ug", [P, 2, 2, DC])
        bd = sb("bd", [P, 2, D])
        u_sb = sb("u_sb", [P, DC, TG])
        s_sb = sb("s_sb", [P, DC, TG])
        g_sb = sb("g_sb", [P, DC, TG])
        y_sb = sb("y_sb", [P, 2, D])
        mp = ctx.enter_context(nc.psum_tensor("mp", [P, 8, 512], FP32))

        r_loaded, e_loaded = sem("r_loaded"), [sem("e_loaded0"), sem("e_loaded1")]
        n2_ready, t2_ready, t2_free = sem("n2_ready"), sem("t2_ready"), sem("t2_free")
        gate_ready, sel_ready, exp_ready = sem("gate_ready"), sem("sel_ready"), sem("exp_ready")
        u_ready, u_done, z_ready, s_done = sem("u_ready"), sem("u_done"), sem("z_ready"), sem("s_done")
        g_done, y_ready, y_done, dve2 = sem("g_done"), sem("y_ready"), sem("y_done"), sem("dve2")
        stored, var_ready, rstd_ready = sem("stored"), sem("var_ready"), sem("rstd_ready")
        block2 = ctx.enter_context(nc.Block())

        def bcast(v, n):
            return v.rearrange("(a n) -> a n", a=1).to_broadcast([P, n])

        @block2.sync
        def _(sp):
            sp.dma_start(wr[:], w_router).then_inc(r_loaded, 16)
            sp.dma_start(brt[:], bcast(b_router, ER)).then_inc(r_loaded, 16)
            sp.dma_start(gbt[:], bcast(gate_bias, ER)).then_inc(r_loaded, 16)

            with sp.Fori(0, E // 2) as pair:
                for h in range(2):
                    e = pair * 2 + h
                    if h == 0:
                        sp.wait_ge(y_done, pair * (2 * TILES))
                    else:
                        sp.wait_ge(y_done, pair * (2 * TILES))
                    sp.dma_start(w_sb[:, h], w_all[bass.ds(e, 1)].rearrange("a p m c n -> p (a m) c n"))\
                      .then_inc(e_loaded[h], 16)
                    sp.dma_start(b_ug[:, h], b_up_gate[bass.ds(e, 1)].rearrange("a p m c -> p (a m) c"))\
                      .then_inc(e_loaded[h], 16)
                    sp.dma_start(bd[:, h, :], b_down[bass.ds(e, 1), :].to_broadcast([P, D]))\
                      .then_inc(e_loaded[h], 16)
            for t in range(0, TILES, BT):
                sp.wait_ge(y_done, (E - 1) * TILES + t + BT)
                sp.dma_start(out.rearrange("(t p) d -> p t d", p=P)[:, t:t + BT, :], x_sb[:, t:t + BT, :])\
                  .then_inc(stored, 16)
            sp.wait_ge(stored, 16 * NG)

        @block2.gpsimd
        def _(pool):
            pool.wait_ge(var_ready, 1)
            nc.gpsimd.tensor_tensor(rsqrt[:], mean_sq[:], power[:], ALU.pow).then_inc(rstd_ready, 1)

        @block2.tensor
        def _(pe):
            for t in range(TILES):
                pe.wait_ge(n2_ready, t + 1)
                if t >= 2:
                    pe.wait_ge(t2_free, t - 1)
                for c in range(DC):
                    last = nc.tensor.transpose(mp[:, t % 2, c * P:(c + 1) * P], x2[:, t % 2, c * P:(c + 1) * P],
                                               ident[:])
                last.then_inc(t2_ready, 1)
            pe.wait_ge(t2_free, TILES)
            pe.wait_ge(r_loaded, 48)
            for t in range(TILES):
                for c in range(DC):
                    last = nc.tensor.matmul(mp[:, 2, t * ER:(t + 1) * ER], xt[:, c, t * P:(t + 1) * P], wr[:, c, :],
                                            start=(c == 0), stop=(c == DC - 1))
            last.then_inc(gate_ready, 1)
            pe.wait_ge(sel_ready, 1)
            with pe.Fori(0, E // 2) as pair:
                for h in range(2):
                    pe.wait_ge(e_loaded[h], pair * 48 + 48)
                    for g in range(NG):
                        n = pair * (8 * NG) + (h * NG + g) * 4
                        for i in range(DC):
                            if h or g:
                                pe.wait_ge(y_done, n - 4 + i + 1)
                            else:
                                pe.wait_ge(y_done, n)
                            for c in range(DC):
                                last = nc.tensor.matmul(mp[:, i, :], w_sb[:, h, 0, c, i * P:(i + 1) * P],
                                                        xt[:, c, g * TG:(g + 1) * TG], start=(c == 0), stop=(c == DC - 1))
                            last.then_inc(u_ready, 1)
                        pe.wait_ge(u_done, n + 4)
                        for i in range(DC):
                            pe.wait_ge(s_done, n)
                            for c in range(DC):
                                last = nc.tensor.matmul(mp[:, 4 + i, :], w_sb[:, h, 1, c, i * P:(i + 1) * P],
                                                        u_sb[:, c, :], start=(c == 0), stop=(c == DC - 1))
                            last.then_inc(z_ready, 1)
                        pe.wait_ge(g_done, n + 4)
                        for j in range(GT):
                            for c in range(DC):
                                last = nc.tensor.matmul(mp[:, j, :], g_sb[:, c, j * P:(j + 1) * P],
                                                        w_sb[:, h, 2, c, :], start=(c == 0), stop=(c == DC - 1))
                            last.then_inc(y_ready, 1)

        @block2.scalar
        def _(act):
            act.wait_ge(sel_ready, 1)
            nc.scalar.activation(lg[:], lg[:], ACT.Exp).then_inc(exp_ready, 1)
            with act.Fori(0, E // 2) as pair:
                for h in range(2):
                    act.wait_ge(e_loaded[h], pair * 48 + 48)
                    for g in range(NG):
                        n = pair * (8 * NG) + (h * NG + g) * 4
                        act.wait_ge(g_done, n)
                        for i in range(DC):
                            act.wait_ge(u_ready, n + i + 1)
                            nc.scalar.activation(u_sb[:, i, :], mp[:, i, :], ACT.Identity,
                                                 bias=b_ug[:, h, 0, i:i + 1]).then_inc(u_done, 1)
                        for i in range(DC):
                            act.wait_ge(z_ready, n + i + 1)
                            nc.scalar.activation(s_sb[:, i, :], mp[:, 4 + i, :], ACT.Silu,
                                                 bias=b_ug[:, h, 1, i:i + 1]).then_inc(s_done, 1)

        @block2.vector
        def _(dve):
            steps = [0]

            def done(ins):
                steps[0] += 1
                ins.then_inc(dve2, 1)
                dve.wait_ge(dve2, steps[0])

            def out_of(t):
                dve.wait_ge(t2_ready, t + 1)
                nc.vector.tensor_copy(xt[:, :, t * P:(t + 1) * P], mp[:, t % 2, :].rearrange(
                    "p (c n) -> p c n", n=P)).then_inc(t2_free, 1)
            for t in range(TILES):
                done(nc.vector.bn_stats(stats[:], x_sb[:, t, :]))
                done(nc.vector.bn_aggr(mv[:, t, :], stats[:]))
            nc.vector.tensor_scalar(mean_sq[:], mv[:, :, 1], LN_EPS, None, ALU.add).then_inc(var_ready, 1)
            dve.wait_ge(rstd_ready, 1)
            for t in range(TILES):
                if t >= 2:
                    out_of(t - 2)
                nc.vector.tensor_scalar(x2[:, t % 2, :], x_sb[:, t, :], mv[:, t, 0:1], rsqrt[:, t:t + 1],
                                        ALU.subtract, ALU.mult).then_inc(n2_ready, 1)
            out_of(TILES - 2)
            out_of(TILES - 1)
            for e in range(ER):
                last = nc.vector.memset(order[:, e:e + 1], float(ER - e))
            nc.vector.memset(probs_e[:, :, ER:], 1.0)
            dve.wait_ge(r_loaded, 48)
            dve.wait_ge(gate_ready, 1)
            whole = [P, TILES, ER]
            done(nc.vector.tensor_tensor(gate[:], mp[:, 2, 0:TILES * ER].rearrange("p (t e) -> p t e", e=ER),
                                         brt[:].unsqueeze(1).to_broadcast(whole), ALU.add))
            done(nc.vector.tensor_tensor(biased[:], gate[:], gbt[:].unsqueeze(1).to_broadcast(whole), ALU.add))
            for k in range(2):
                done(nc.vector.tensor_reduce(top[:], biased[:], axis=AX.X, op=ALU.max))
                done(nc.vector.tensor_tensor(key[:], biased[:], top[:].unsqueeze(2).to_broadcast(whole), ALU.is_equal))
                done(nc.vector.tensor_tensor(key[:], key[:], order[:].unsqueeze(1).to_broadcast(whole), ALU.mult))
                done(nc.vector.tensor_reduce(top[:], key[:], axis=AX.X, op=ALU.max))
                done(nc.vector.tensor_tensor(hot[:, k], key[:], top[:].unsqueeze(2).to_broadcast(whole), ALU.is_equal))
                done(nc.vector.tensor_tensor(key[:], hot[:, k], gate[:], ALU.mult))
                done(nc.vector.tensor_reduce(lg[:, k, :], key[:], axis=AX.X, op=ALU.add))
                if k == 0:
                    done(nc.vector.scalar_tensor_tensor(biased[:], hot[:, 0], -3e38, biased[:], ALU.mult, ALU.add))
            done(nc.vector.tensor_tensor(top[:], lg[:, 0, :], lg[:, 1, :], ALU.max))
            nc.vector.tensor_tensor(lg[:], lg[:], top[:].unsqueeze(1).to_broadcast([P, 2, TILES]), ALU.subtract)\
              .then_inc(sel_ready, 1)
            dve.wait_ge(exp_ready, 1)
            done(nc.vector.tensor_tensor(top[:], lg[:, 0, :], lg[:, 1, :], ALU.add))
            done(nc.vector.reciprocal(top[:], top[:]))
            done(nc.vector.tensor_tensor(lg[:], lg[:], top[:].unsqueeze(1).to_broadcast([P, 2, TILES]), ALU.mult))
            for k in range(2):
                done(nc.vector.tensor_tensor(hot[:, k], hot[:, k], lg[:, k, :].unsqueeze(2).to_broadcast(whole),
                                             ALU.mult))
            done(nc.vector.tensor_tensor(probs_e[:, :, 0:ER], hot[:, 0], hot[:, 1], ALU.add))
            base = steps[0]
            with dve.Fori(0, E // 2) as pair:
                for h in range(2):
                    dve.wait_ge(e_loaded[h], pair * 48 + 48)
                    for g in range(NG):
                        n = pair * (8 * NG) + (h * NG + g) * 4
                        for i in range(DC):
                            dve.wait_ge(s_done, n + i + 1)
                            nc.vector.tensor_tensor(g_sb[:, i, :], s_sb[:, i, :], u_sb[:, i, :], ALU.mult)\
                              .then_inc(g_done, 1)
                        for j in range(GT):
                            t = g * GT + j
                            dve.wait_ge(y_ready, n + j + 1)
                            nc.vector.tensor_tensor(y_sb[:, j % 2, :], mp[:, j, :], bd[:, h, :], ALU.add)\
                              .then_inc(dve2, 1)
                            dve.wait_ge(dve2, n + j + 1 + base)
                            nc.vector.scalar_tensor_tensor(x_sb[:, t, :], y_sb[:, j % 2, :],
                                                           probs_e[:, t, bass.ds(pair * 2 + h, 1)], x_sb[:, t, :],
                                                           ALU.mult, ALU.add).then_inc(y_done, 1)


def kernel(**inputs):
    import numpy as np
    import concourse.bacc as bacc
    from concourse.bass_utils import run_bass_kernel_spmd

    nc = bacc.Bacc("TRN2", target_bir_lowering=False, num_devices=1)
    a = {k.replace("L0_", ""): np.asarray(v) for k, v in inputs.items()}
    x, context = a["x"], a["ctx_2048"]
    d = x.shape[-1]
    kv = np.concatenate([a["xattn_Wk"], a["xattn_Wv"]], axis=0)
    wk, wv = kv[0::2].T.reshape(d, -1, 1, P), kv[1::2].T.reshape(d, -1, 1, P)
    f = {n: a["ffn_" + n] for n in ("Wr", "br", "gate_bias", "Wup", "bup", "Wgate", "bgate", "Wdown", "bdown",
                                    "Wsu", "bsu", "Wsg", "bsg", "Wsd", "bsd")}
    w = np.stack([np.concatenate([f[r], f[s][None]]) for r, s in (("Wup", "Wsu"), ("Wgate", "Wsg"),
                                                                   ("Wdown", "Wsd"))], axis=1)
    b = np.stack([np.concatenate([f[r], f[s][None]]) for r, s in (("bup", "bsu"), ("bgate", "bsg"))], axis=1)
    arrays = {
        "x": x.reshape(-1, d),
        "ctx_t": context.transpose(0, 2, 1),
        "wq_t": a["xattn_Wq"].T,
        "wkv_t": np.concatenate([wk, wv], axis=2).reshape(d, -1),
        "w_all": w.reshape(w.shape[0], 3, d // P, P, d).transpose(0, 3, 1, 2, 4),
        "b_up_gate": b.reshape(b.shape[0], 2, d // P, P).transpose(0, 3, 1, 2),
        "b_down": np.concatenate([f["bdown"], f["bsd"][None]]),
        "w_router": f["Wr"].reshape(d // P, P, -1).transpose(1, 0, 2),
        "b_router": f["br"],
        "gate_bias": f["gate_bias"],
    }
    arrays = {k: np.ascontiguousarray(v) for k, v in arrays.items()}
    args = [nc.dram_tensor(k, v.shape, mybir.dt.from_np(v.dtype), kind="ExternalInput").ap()
            for k, v in arrays.items()]
    out = nc.dram_tensor("out", arrays["x"].shape, FP32, kind="ExternalOutput").ap()
    moe_layer(nc, *args, out)
    r = run_bass_kernel_spmd(nc, [arrays], core_ids=[0])
    return r.results[0]["out"].reshape(x.shape)
```

```python
from contextlib import ExitStack

import concourse.bass as bass
from concourse import mybir

FP32 = mybir.dt.float32
FP32R = mybir.dt.float32r
ALU = mybir.AluOpType
ACT = mybir.ActivationFunctionType
AX = mybir.AxisListType

P = 128


class Tally:

    def __init__(self, sem):
        self.sem, self.const, self.turns = sem, 0, 0

    def next(self, by=1):
        self.const += by
        return self.now()

    def now(self, less=0):
        return self.turns + (self.const - less)

    def past(self, n):
        return not isinstance(self.turns, int) or self.const > n


def moe_layer(nc, x, ctx_t, wq_t, wkv_t, w_all, b_up_gate, b_down, w_router, b_router, gate_bias, xn_dram, y_dram,
              out):
    TOKENS, D = x.shape
    BATCH = ctx_t.shape[0]
    SEQ = TOKENS // BATCH
    CTX = ctx_t.shape[2]
    DC = D // P
    HD = 16
    TILES = TOKENS // P
    BT = SEQ // P
    MT = CTX // P
    GROUPS = DC
    GH = P // HD
    PAIRS = GH // 2
    ER = w_router.shape[2]
    LN_EPS, RMS_EPS = 1e-5, 1e-6

    with ExitStack() as ctx:
        att = ExitStack()
        def sb(name, shape, dt=FP32):
            return ctx.enter_context(nc.sbuf_tensor(name, shape, dt))

        def ps(name, shape):
            return att.enter_context(nc.psum_tensor(name, shape, FP32))

        def sem(name):
            return ctx.enter_context(nc.semaphore(name))

        x_sb = sb("x_sb", [P, TILES, D])
        ident = sb("ident", [P, P])
        w_raw = sb("w_raw", [P, 3, DC, D])
        raw_loaded = [sem(f"raw_loaded{m}") for m in range(3)]
        stats = sb("stats", [P, 6])
        mv = sb("mv", [P, TILES, 2])
        rstd = sb("rstd", [P, TILES])
        power = sb("power", [P, 2 * 8])
        mean_sq = sb("mean_sq", [P, 2, 2 * 8])
        rsqrt = sb("rsqrt", [P, 2, 2 * 8])

        def asb(name, shape, dt=FP32):
            return att.enter_context(nc.sbuf_tensor(name, shape, dt))

        wq = asb("wq", [P, DC, D])
        wkv = asb("wkv", [P, DC, GROUPS, 2 * P])
        ctx_sb = asb("ctx_sb", [P, DC, CTX])
        xn_t = asb("xn_t", [P, DC, SEQ])
        xn = asb("xn", [P, 2, D])
        raw = asb("raw", [P, 2, 2 * GH, HD])
        sq = asb("sq", [P, 2 * GH, HD])
        qn = asb("qn", [P, 2, 2 * GH, HD])
        split = asb("split", [P, 2, 2, GH, 4, HD])
        q_stack = asb("q_stack", [P, 2, PAIRS, SEQ], FP32R)
        k_stack = asb("k_stack", [P, 2, PAIRS, CTX], FP32R)
        v_sb = asb("v_sb", [P, 2, MT, GH, 2 * HD])
        probs = asb("probs", [P, 2, 4, SEQ])
        o_sb = asb("o_sb", [P, SEQ])
        o_n = asb("o_n", [P, BT, 4, HD])
        rec = asb("rec", [P, BT, 4])
        zeros = asb("zeros", [P, 1, D])

        scores = ps("scores", [P, 2, 2, SEQ])
        o_ps = ps("o_ps", [P, SEQ])
        pj = ps("pj", [P, 512])
        tr = ps("tr", [P, 2, 512])

        w_loaded = sem("w_loaded")
        x_first = sem("x_first")
        x_rest = sem("x_rest")
        ctx_loaded = sem("ctx_loaded")
        ones_set = sem("ones_set")
        ident_zero = sem("ident_zero")
        zeros_set, y_filled = sem("zeros_set"), sem("y_filled")
        ident_set = sem("ident_set")
        xn_ready = sem("xn_ready")
        tr_ready = sem("tr_ready")
        tr_free = sem("tr_free")
        pj_ready = sem("pj_ready")
        pj_free = sem("pj_free")
        split_ready = sem("split_ready")
        sc_ready = sem("sc_ready")
        p_ready = sem("p_ready")
        pv_done = sem("pv_done")
        o_ready = sem("o_ready")
        o_evac = sem("o_evac")
        dve_step = sem("dve_step")
        mean_ready = sem("mean_ready")
        power_set = sem("power_set")
        rsqrt_ready = sem("rsqrt_ready")

        block = att.enter_context(nc.Block())

        def loop_over_batches(engine, tallies, turn):
            with engine.Fori(1, BATCH) as r:
                before = [t.const for t in tallies]
                per_turn = [TURN[t.sem.name] for t in tallies]
                for t, n in zip(tallies, per_turn):
                    t.turns = (r - 1) * n
                turn(r)
            for t, n, was in zip(tallies, per_turn, before):
                assert t.const - was == n, (t.sem.name, t.const - was)
                t.turns = 0
                t.const += n * (BATCH - 2)

        TURN = {"xn_ready": BT, "tr_ready": BT + 4 * (2 * BT + 2), "tr_free": BT + 4 * (2 * BT + 2),
                "pj_ready": 4 * BT, "pj_free": 4 * BT, "split_ready": 4 * BT, "sc_ready": 4 * 16,
                "p_ready": 4 * 16, "pv_done": 4 * 8, "o_ready": 8, "o_evac": 8,
                "dve_step": 8 * 1 + 16 * 5,
                "rsqrt_ready": 4 * BT}

        PROJECTIONS = {0: 0, 1: 1, 2: 2, 3: 3}
        SPLITS = {2: 0, 3: 1, 4: 2, 5: 3}
        STACKS = {3: 0, 4: 1, 5: 2, 6: 3}

        @block.gpsimd
        def _(pool):
            nc.gpsimd.memset(ident[:], 0.0).then_inc(ident_zero, 1)
            nc.gpsimd.memset(zeros[:], 0.0).then_inc(zeros_set, 1)
            nc.gpsimd.memset(v_sb[:, :, :, :, HD:], 1.0).then_inc(ones_set, 1)
            pool.wait_ge(ident_zero, 1)
            nc.gpsimd.affine_select(out=ident[:], in_=ident[:], compare_op=ALU.not_equal, fill=1.0, base=0,
                                    pattern=[[-1, P]], channel_multiplier=1).then_inc(ident_set, 1)
            nc.gpsimd.memset(power[:], -0.5).then_inc(power_set, 1)
            pool.wait_ge(power_set, 1)

            def root(n, half):
                pool.wait_ge(mean_ready, n + 1)
                nc.gpsimd.tensor_tensor(rsqrt[:, half], mean_sq[:, half], power[:], ALU.pow)\
                  .then_inc(rsqrt_ready, 1)
            root(0, 0)
            with pool.Fori(0, GROUPS * BT // 2) as i:
                root(i * 2 + 1, 0)
                root(i * 2 + 2, 1)
            root(GROUPS * BT + 1, 0)
            with pool.Fori(0, GROUPS * (TILES - BT) // 2) as i:
                root(i * 2 + (GROUPS * BT + 2), 0)
                root(i * 2 + (GROUPS * BT + 3), 1)

        @block.sync
        def _(sp):
            x_v = x.rearrange("(t p) d -> p t d", p=P)
            sp.dma_start(x_sb[:, 0:BT, :], x_v[:, 0:BT, :]).then_inc(x_first, 16)
            sp.dma_start(wq[:], wq_t.rearrange("(c p) n -> p c n", p=P)).then_inc(w_loaded, 16)
            sp.dma_start(ctx_sb[:], ctx_t[0, :, :].rearrange("(c p) m -> p c m", p=P)).then_inc(ctx_loaded, 16)
            sp.dma_start(wkv[:], wkv_t.rearrange("(c p) (g n) -> p c g n", p=P, n=2 * P)).then_inc(w_loaded, 16)
            sp.dma_start(x_sb[:, BT:, :], x_v[:, BT:, :]).then_inc(x_rest, 16)
            for m in range(3):
                sp.dma_start(w_raw[:, m], w_all[0, :, m]).then_inc(raw_loaded[m], 16)
            sp.wait_ge(zeros_set, 1)
            fill = y_dram[2 * TOKENS:, :].rearrange("(s p) d -> p s d", p=P)
            sp.dma_start(fill, zeros[:].to_broadcast([P, fill.shape[1], D])).then_inc(y_filled, 16)
            with sp.Fori(1, BATCH) as b:
                sp.wait_ge(pj_ready, b * (GROUPS * BT))
                sp.dma_start(ctx_sb[:], ctx_t[bass.ds(b, 1), :, :].rearrange("a (c p) m -> p (a c) m", p=P))\
                  .then_inc(ctx_loaded, 16)
            sp.wait_ge(y_filled, 16)

        @block.tensor
        def _(pe):
            xn_r, trr, trf = Tally(xn_ready), Tally(tr_ready), Tally(tr_free)
            pjr, spl = Tally(pj_ready), Tally(split_ready)
            scr, pvd, orr = Tally(sc_ready), Tally(pv_done), Tally(o_ready)
            tallies = [xn_r, trr, pjr, spl, scr, pvd, orr]

            def transposes(sources):
                trr.next()
                if trr.past(2):
                    pe.wait_ge(tr_free, trr.now(2))
                for i, src in enumerate(sources):
                    last = nc.tensor.transpose(tr[:, trr.const % 2, i * P:(i + 1) * P], src, ident[:])
                last.then_inc(tr_ready, 1)

            def norm_transposes(t):
                pe.wait_ge(xn_ready, xn_r.next())
                transposes([xn[:, t % 2, c * P:(c + 1) * P] for c in range(DC)])

            def project(g, t, batch):
                if batch is not None:
                    pe.wait_ge(ctx_loaded, batch * 16 + 16)
                    pe.wait_ge(tr_free, trr.now())
                pjr.next()
                if pjr.past(1):
                    pe.wait_ge(pj_free, pjr.now(1))
                for c in range(DC):
                    nc.tensor.matmul(pj[:, 0:P], xn_t[:, c, t * P:(t + 1) * P], wq[:, c, g * P:(g + 1) * P],
                                     start=(c == 0), stop=(c == DC - 1))
                for c in range(DC):
                    last = nc.tensor.matmul(pj[:, P:3 * P], ctx_sb[:, c, t * P:(t + 1) * P], wkv[:, c, g, :],
                                            start=(c == 0), stop=(c == DC - 1))
                last.then_inc(pj_ready, 1)

            def stack_transposes(t):
                pe.wait_ge(split_ready, spl.next())
                for qk in range(2):
                    rows = split[:, t % 2, qk].rearrange("p h s d -> p (h s d)")
                    transposes([rows[:, i * P:(i + 1) * P] for i in range(PAIRS)])

            def score(par, s):
                g4, mt = divmod(s, MT)
                for a in range(2):
                    scr.next()
                    if scr.past(2):
                        pe.wait_ge(p_ready, scr.now(2))
                    hp = g4 * 2 + a
                    for i in range(2):
                        rows = slice(64 * i, 64 * i + 64)
                        last = nc.tensor.matmul(scores[:, a, i, :], k_stack[rows, par, hp, mt * P:(mt + 1) * P],
                                                q_stack[rows, par, hp, :], start=True, stop=True)
                    last.then_inc(sc_ready, 1)

            def weigh(par, s, behind):
                g4, mt = divmod(s, MT)
                pe.wait_ge(p_ready, scr.now(behind))
                if mt == 0:
                    if orr.past(0):
                        pe.wait_ge(o_evac, orr.now())
                for j in range(4):
                    last = nc.tensor.matmul(o_ps[32 * j:32 * j + 32, :], v_sb[:, par, mt, 4 * g4 + j, :],
                                            probs[:, s % 2, j, :], start=(mt == 0), stop=(mt == MT - 1))
                pvd.next()
                last.then_inc(pv_done, 1)
                if mt == MT - 1:
                    orr.next()

            def out_transposes():
                pe.wait_ge(o_evac, orr.now())
                transposes([o_sb[:, t * P:(t + 1) * P] for t in range(BT)])

            def unit(k, batch, first=False, last=False):
                par, nxt = k % 2, (k + 1) % GROUPS
                new_batch = k == GROUPS - 1 and not last
                for s in range(8):
                    if s == 0:
                        pe.wait_ge(tr_free, trr.now())
                        if new_batch:
                            norm_transposes(0)
                    score(par, s)
                    if not last and s in PROJECTIONS:
                        project(nxt, PROJECTIONS[s], batch + 1 if new_batch else None)
                    if not last and s in STACKS:
                        stack_transposes(STACKS[s])
                    if s:
                        weigh(par, s - 1, 2)
                    elif not first:
                        weigh(1 - par, 7, 2)
                    if s == 5 or (s == 1 and not first):
                        out_transposes()
                    if new_batch and s + 1 in PROJECTIONS:
                        norm_transposes(PROJECTIONS[s + 1])

            pe.wait_ge(ident_set, 1)
            pe.wait_ge(ones_set, 1)
            pe.wait_ge(w_loaded, 32)
            for t in range(BT):
                norm_transposes(t)
                project(0, t, 0)
                if t:
                    stack_transposes(t - 1)
            stack_transposes(BT - 1)
            unit(0, 0, first=True)
            unit(1, 0)
            unit(2, 0)

            def turn(r):
                unit(3, r - 1)
                for k in range(3):
                    unit(k, r)
            loop_over_batches(pe, tallies, turn)
            unit(3, BATCH - 1, last=True)
            weigh(1, 7, 0)
            out_transposes()

        @block.scalar
        def _(act):
            scr, steps = Tally(sc_ready), Tally(pv_done)

            def unit():
                for s in range(8):
                    for a in range(2):
                        act.wait_ge(sc_ready, scr.next())
                        if a == 0 and steps.past(1):
                            act.wait_ge(pv_done, steps.now(1))
                        nc.scalar.activation(probs[:, s % 2, 2 * a:2 * a + 2, :], scores[:, a], ACT.Exp,
                                             scale=float(HD) ** 0.5).then_inc(p_ready, 1)
                    steps.next()

            for _ in range(3):
                unit()

            def turn(r):
                for _ in range(4):
                    unit()
            loop_over_batches(act, [scr, steps], turn)
            unit()

        @block.vector
        def _(dve):
            trr, pjr, orr, step = Tally(tr_ready), Tally(pj_ready), Tally(o_ready), Tally(dve_step)
            rsq = Tally(rsqrt_ready)
            tallies = [trr, pjr, orr, step, rsq]

            def done(ins):
                ins.then_inc(dve_step, 1)
                dve.wait_ge(dve_step, step.next())

            def root():
                dve.wait_ge(rsqrt_ready, rsq.next())

            def stat(t):
                done(nc.vector.bn_stats(stats[:], x_sb[:, t, :]))
                done(nc.vector.bn_aggr(mv[:, t, :], stats[:]))

            def deviations(tiles):
                nc.vector.tensor_scalar(mean_sq[:, 0, tiles], mv[:, tiles, 1], LN_EPS, None, ALU.add)\
                  .then_inc(mean_ready, 1)
                root()
                done(nc.vector.tensor_copy(rstd[:, tiles], rsqrt[:, 0, tiles]))

            def norm(batch, t):
                tile = batch * BT + t
                nc.vector.tensor_scalar(xn[:, t % 2, :], x_sb[:, tile, :], mv[:, tile, 0:1], rstd[:, tile:tile + 1]
                                        if isinstance(tile, int) else rstd[:, bass.ds(tile, 1)],
                                        ALU.subtract, ALU.mult).then_inc(xn_ready, 1)

            def evacuate(dst):
                dve.wait_ge(tr_ready, trr.next())
                src = tr[:, trr.const % 2, :].rearrange("p (a b) -> p a b", b=P)
                nc.vector.tensor_copy(dst, src).then_inc(tr_free, 1)

            def norm_out(t):
                evacuate(xn_t[:, :, t * P:(t + 1) * P])

            def project_out(par, t):
                dve.wait_ge(pj_ready, pjr.next())
                done(nc.vector.tensor_copy(raw[:, t % 2], pj[:, 0:2 * P].rearrange("p (h d) -> p h d", d=HD)))
                done(nc.vector.tensor_tensor(sq[:], raw[:, t % 2], raw[:, t % 2], ALU.mult))
                sums = mean_sq[:, t % 2]
                done(nc.vector.tensor_reduce(sums, sq[:], axis=AX.X, op=ALU.add))
                nc.vector.tensor_scalar(sums, sums, HD * RMS_EPS, None, ALU.add).then_inc(mean_ready, 1)
                nc.vector.tensor_copy(v_sb[:, par, t, :, 0:HD], pj[:, 2 * P:3 * P].rearrange(
                    "p (h d) -> p h d", d=HD)).then_inc(pj_free, 1)

            def split_out(t):
                root()
                done(nc.vector.tensor_tensor(qn[:, t % 2], raw[:, t % 2], rsqrt[:, t % 2].unsqueeze(2)
                                             .to_broadcast([P, 2 * GH, HD]), ALU.mult))
                q, k = split[:, t % 2, 0], split[:, t % 2, 1]
                twice = [P, GH, 2, HD]
                q_in = qn[:, t % 2, 0:GH, :].unsqueeze(2).to_broadcast(twice)
                k_in = qn[:, t % 2, GH:, :].unsqueeze(2).to_broadcast(twice)
                nc.vector.tensor_copy(q[:, :, 0:2, :].bitcast(FP32R), q_in)
                done(nc.vector.tensor_copy(k[:, :, 0:4:2, :].bitcast(FP32R), k_in))
                nc.vector.tensor_tensor(q[:, :, 2:4, :].bitcast(FP32R), q_in, q[:, :, 0:2, :], ALU.subtract)
                nc.vector.tensor_tensor(k[:, :, 1:4:2, :].bitcast(FP32R), k_in, k[:, :, 0:4:2, :], ALU.subtract)\
                  .then_inc(split_ready, 1)

            def stacks_out(par, t):
                evacuate(q_stack[:, par, :, t * P:(t + 1) * P])
                evacuate(k_stack[:, par, :, t * P:(t + 1) * P])

            def group_out():
                dve.wait_ge(pv_done, orr.next() * MT)
                nc.vector.tensor_copy(o_sb[:], o_ps[:]).then_inc(o_evac, 1)

            def finalize(batch, g, g4):
                dve.wait_ge(tr_ready, trr.next())
                o_t = tr[:, trr.const % 2, :].rearrange("p (t h d) -> p t h d", t=BT, d=2 * HD)
                done(nc.vector.reciprocal(rec[:], o_t[:, :, :, HD]))
                nc.vector.tensor_tensor(o_n[:], o_t[:, :, :, 0:HD],
                                        rec[:].unsqueeze(3).to_broadcast([P, BT, 4, HD]), ALU.mult)\
                  .then_inc(tr_free, 1)
                dve.wait_ge(tr_free, trr.now())
                cols = g * P + g4 * 4 * HD
                xs = x_sb[:, bass.ds(batch * BT, BT), cols:cols + 4 * HD]
                nc.vector.tensor_tensor(xs, xs, o_n[:].rearrange("p t h d -> p t (h d)"), ALU.add)

            def unit(k, batch, first=False, last=False, between=None):
                par = k % 2
                new_batch = k == GROUPS - 1 and not last
                before = (batch, k - 1) if k else (batch - 1, GROUPS - 1)
                for s in range(8):
                    if new_batch and s == 0:
                        norm(batch + 1, 0)
                        norm(batch + 1, 1)
                    if new_batch and s == 0:
                        norm_out(0)
                        norm(batch + 1, 2)
                    if not last and s in SPLITS:
                        split_out(SPLITS[s])
                    if not last and s in PROJECTIONS:
                        project_out(1 - par, PROJECTIONS[s])
                    if not last and s in STACKS:
                        stacks_out(1 - par, STACKS[s])
                    if s == 4 or (s == 0 and not first):
                        group_out()
                    if s == 1 and not first:
                        finalize(*before, 1)
                    if s == 5:
                        finalize(batch, k, 0)
                    if new_batch and s + 1 in PROJECTIONS:
                        t = PROJECTIONS[s + 1]
                        norm_out(t)
                        if t + 2 < BT:
                            norm(batch + 1, t + 2)
                    if between:
                        between(s)

            nc.vector.memset(mean_sq[:], 1.0)
            dve.wait_ge(x_first, 16)
            for t in range(BT):
                stat(t)
            deviations(slice(0, BT))
            norm(0, 0)
            norm(0, 1)
            for t in range(BT):
                norm_out(t)
                if t + 2 < BT:
                    norm(0, t + 2)
                if t:
                    split_out(t - 1)
                project_out(0, t)
                if t:
                    stacks_out(0, t - 1)
            split_out(BT - 1)
            stacks_out(0, BT - 1)
            unit(0, 0, first=True)
            dve.wait_ge(x_rest, 16)
            unit(1, 0, between=lambda s: stat(BT + s))
            unit(2, 0, between=lambda s: stat(BT + 8 + s) if s < TILES - BT - 8 else None)
            deviations(slice(BT, TILES))

            def turn(r):
                unit(3, r - 1)
                for k in range(3):
                    unit(k, r)
            loop_over_batches(dve, tallies, turn)
            unit(3, BATCH - 1, last=True)
            group_out()
            finalize(BATCH - 1, GROUPS - 1, 1)

        att.close()

        TS = 2 * P
        NS = TOKENS // TS
        NA = 5
        NB = NS - NA
        MOST = 2 * TOKENS // TS + ER
        COLS = 2 * (MOST + NB)
        LISTED = [(k, t) for k in range(2) for t in range(TILES)] + [(2, t) for t in range(2 * NA, TILES)]
        PART = len(LISTED) // 2
        FP16, INT32 = mybir.dt.float16, mybir.dt.int32

        w_sb = sb("w_sb", [P, 2, 2, 3, DC, D], FP32R)
        b_ug = sb("b_ug", [P, 2, 2, DC])
        bd = sb("bd", [P, 2, D])
        xg = sb("xg", [P, 2, D])
        x_hi, x_lo = sb("x_hi", [P, DC, TS], FP32R), sb("x_lo", [P, DC, TS], FP32R)
        u_hi, u_lo = sb("u_hi", [P, DC, TS], FP32R), sb("u_lo", [P, DC, TS], FP32R)
        s_sb, g_sb = sb("s_sb", [P, DC, TS]), sb("g_sb", [P, DC, TS])
        g_hi, g_lo = sb("g_hi", [P, DC, TS], FP32R), sb("g_lo", [P, DC, TS], FP32R)
        y_sb = sb("y_sb", [P, 2, D])
        wr = sb("wr", [P, DC, ER])
        brt, gbt = sb("brt", [P, ER]), sb("gbt", [P, ER])
        whole = [P, TILES, ER]
        gate, biased, key, picked = (sb(n, whole) for n in ("gate", "biased", "key", "picked"))
        hot = sb("hot", [P, 2, TILES, ER])
        order, top = sb("order", [P, ER]), sb("top", [P, TILES])
        prob = sb("prob", [P, 2, TILES])
        before = sb("before", [P, P])
        ones = sb("ones", [P, P])
        prefix = sb("prefix", [P, 2, TILES, ER])
        counts = sb("counts", [P, TILES + 1, ER])
        tiles_i, tiles_f = sb("tiles_i", [P, ER], INT32), sb("tiles_f", [P, ER])
        start_f, start_i = sb("start_f", [P, ER + 1]), sb("start_i", [P, ER + 1], INT32)
        pos_f, pos_i = sb("pos_f", [P, 3, TILES]), sb("pos_i", [P, 3, TILES], INT32)
        col_i, col_f = sb("col_i", [P, 3, TILES], INT32), sb("col_f", [P, 3, TILES])
        row_f = sb("row_f", [P, 3, TILES])
        iota_i, iota_f = sb("iota_i", [P, P], INT32), sb("iota_f", [P, P])
        token_i, token = sb("token_i", [P, TILES], INT32), sb("token", [P, TILES])
        hot_row, hot_col = sb("hot_row", [P, PART, P], FP16), sb("hot_col", [P, PART, COLS], FP16)
        table_f, table = sb("table_f", [P, COLS]), sb("table", [P, COLS], INT32)
        index = sb("index", [P, 2], INT32)
        yg = w_raw[:].rearrange("p m c n -> p (m c) n")
        RING = 3 * DC

        def two_banks(name):
            return ctx.enter_context(nc.psum_tensor(name, [P, 2, 2, TS], FP32))
        xt_ps, u_ps, z_ps, y_ps = two_banks("xt_ps"), two_banks("u_ps"), two_banks("z_ps"), two_banks("y_ps")
        y_v = y_ps[:].rearrange("p j a n -> p j (a n)")

        r_loaded, b_loaded = sem("r_loaded"), [sem("b_loaded0"), sem("b_loaded1")]
        var_ready, rstd_ready, n2_ready = sem("var_ready"), sem("rstd_ready"), sem("n2_ready")
        n2_stored = [sem("n2_stored0"), sem("n2_stored1")]
        t2_ready, t2_done, gate_part, sel_ready, exp_ready = (
            sem(n) for n in ("t2_ready", "t2_done", "gate_part", "sel_ready", "exp_ready"))
        iota_set, before_set, picked_ready, window_ready, window_read = (
            sem(n) for n in ("iota_set", "before_set", "picked_ready", "window_ready", "window_read"))
        start_ready, hots_ready, table_ready, index_ready = (
            sem(n) for n in ("start_ready", "hots_ready", "table_ready", "index_ready"))
        xg_loaded, xt_ready, xh_done, xl_done = (sem(n) for n in ("xg_loaded", "xt_ready", "xh_done", "xl_done"))
        u_ready, uh_done, ul_done, z_ready, s_done = (
            sem(n) for n in ("u_ready", "uh_done", "ul_done", "z_ready", "s_done"))
        g_done, gh_done, gl_done, y_ready, y_done = (
            sem(n) for n in ("g_done", "gh_done", "gl_done", "y_ready", "y_done"))
        y_stored, hi_done, lo_done = (
            sem(n) for n in ("y_stored", "hi_done", "lo_done"))
        yg_loaded = [sem(f"yg_loaded{i}") for i in range(RING)]
        added, out_stored, dve2 = sem("added"), sem("out_stored"), sem("dve2")
        block2 = ctx.enter_context(nc.Block())

        def bcast(v, n):
            return v.rearrange("(a n) -> a n", a=1).to_broadcast([P, n])

        passed = sem("passed")

        def routed(engine, head, tile):
            engine.wait_ge(start_ready, 1)

            def start_of(e):
                at = start_i[0:1, e:e + 1] if isinstance(e, int) else start_i[0:1, bass.ds(e, 1)]
                return engine.value_load(at, min_val=0, max_val=MOST)

            def expert(j, par, nth, first, end):
                head(j, par, nth, first + NA)
                with engine.Fori(first, end) as i:
                    tile(i + NA, par)

            with engine.Fori(0, ER // 2) as pair:
                s0, s1, s2 = start_of(pair * 2), start_of(pair * 2 + 1), start_of(pair * 2 + 2)
                expert(pair * 2 + 1, 1, pair, s0, s1)
                expert(pair * 2 + 2, 0, pair + 1, s1, s2)
            s0, s1 = start_of(ER - 1), start_of(ER)
            expert(ER, 1, ER // 2, s0, s1)
            return s1

        @block2.sync
        def _(sp):
            sp.dma_start(wr[:], w_router).then_inc(r_loaded, 16)
            sp.dma_start(brt[:], bcast(b_router, ER)).then_inc(r_loaded, 16)
            sp.dma_start(gbt[:], bcast(gate_bias, ER)).then_inc(r_loaded, 16)

            def load_weights(j):
                for m in range(3):
                    sp.dma_start(w_raw[:, m], w_all[bass.ds(j, 1), :, m].rearrange("a p c n -> p (a c) n"))\
                      .then_inc(raw_loaded[m], 16)

            def load_biases(j, par):
                sp.dma_start(b_ug[:, par], b_up_gate[bass.ds(j, 1)].rearrange("a p m c -> p (a m) c"))\
                  .then_inc(b_loaded[par], 16)
                sp.dma_start(bd[:, par, :], b_down[bass.ds(j, 1), :].to_broadcast([P, D])).then_inc(b_loaded[par], 16)

            load_biases(0, 0)
            load_biases(1, 1)
            sp.wait_ge(lo_done, 3)
            load_weights(1)
            for t in range(TILES):
                sp.wait_ge(n2_ready, t + 1)
                sp.dma_start(xn_dram.rearrange("(t p) d -> p t d", p=P)[:, t, :], xg[:, t % 2, :])\
                  .then_inc(n2_stored[t % 2], 16)
            sp.wait_ge(lo_done, 6)
            load_weights(2)

            def head(j, par, nth, first):
                sp.wait_ge(y_done, first * 2)
                load_biases(j + 1, 1 - par)
                if not isinstance(j, int):
                    sp.wait_ge(lo_done, j * 3 + 6)
                    load_weights(j + 2)

            def tile(n, par):
                for h in range(2):
                    sp.wait_ge(y_done, n * 2 + h + 1)
                    sp.dma_start(y_dram.rearrange("(s p) d -> p s d", p=P)[:, bass.ds((n - NA) * 2 + h, 1), :],
                                 y_sb[:, h:h + 1, :]).then_inc(y_stored, 16)
            routed(sp, head, tile)
            for t in range(TILES):
                sp.wait_ge(added, 2 * t + 2)
                sp.dma_start(out.rearrange("(t p) d -> p t d", p=P)[:, t, :], x_sb[:, t, :]).then_inc(out_stored, 16)
            sp.wait_ge(out_stored, 16 * TILES)

        def weight_parts(j):
            return (j + 1) * 16

        @block2.gpsimd
        def _(pool):
            pool.wait_ge(var_ready, 1)
            nc.gpsimd.tensor_tensor(rsqrt[:, 0], mean_sq[:, 0], power[:], ALU.pow).then_inc(rstd_ready, 1)
            nc.gpsimd.iota(iota_i[:], [[1, P]], base=0, channel_multiplier=0).then_inc(iota_set, 1)
            nc.gpsimd.iota(token_i[:], [[P, TILES]], base=0, channel_multiplier=1).then_inc(iota_set, 1)
            nc.gpsimd.memset(ones[:], 1.0).then_inc(before_set, 1)
            pool.wait_ge(before_set, 1)
            nc.gpsimd.affine_select(out=before[:], in_=ones[:], compare_op=ALU.is_gt, fill=0.0, base=0,
                                    pattern=[[1, P]], channel_multiplier=-1).then_inc(before_set, 1)

            def rows(n):
                if n:
                    pool.wait_ge(xt_ready, 2 * n)
                for h in range(2):
                    pool.dma_start(xg[:, h, :], xn_dram.rearrange("(t p) d -> p t d", p=P)[:, 2 * n + h, :])\
                        .then_inc(xg_loaded, 16)

            def gather(n):
                pool.wait_ge(xt_ready, n * 2)
                pool.wait_ge(table_ready, 1)
                nc.gpsimd.tensor_copy(index[:], table[:, bass.ds((n - NA) * 2, 2)]).then_inc(index_ready, 1)
                pool.wait_ge(index_ready, n - NA + 1)
                pool.sem_inc(passed)
                for h in range(2):
                    nc.gpsimd.indirect_dma_start(
                        out=xg[:, h, :], out_offset=None, in_=xn_dram,
                        in_offset=bass.IndirectOffsetOnAxis(ap=index[:, h:h + 1].bitcast(mybir.dt.uint32), axis=0),
                        ).then_inc(xg_loaded, 16)

            for par in range(2):
                pool.wait_ge(n2_stored[par], 16 * TILES // 2)
            pool.wait_ge(t2_ready, TILES)
            for n in range(NA):
                rows(n)
            gather(NA)

            total = routed(pool, lambda j, par, nth, first: None, lambda n, par: gather(n + 1))

            def result(m):
                if m >= RING:
                    pool.wait_ge(added, m - RING + 1)
                nc.gpsimd.indirect_dma_start(
                    out=yg[:, m % RING, :], out_offset=None, in_=y_dram,
                    in_offset=bass.IndirectOffsetOnAxis(
                        ap=pos_i[:, m % 2, m // 2:m // 2 + 1].bitcast(mybir.dt.uint32), axis=0),
                    ).then_inc(yg_loaded[m % RING], 16)

            gather(total + NA + 1)
            pool.wait_ge(y_stored, total * 32)
            pool.sem_inc(passed)
            pool.wait_ge(lo_done, 3 * (ER + 2))
            for m in range(10):
                result(m)
            gather(total + NA + 2)
            for m in range(10, 2 * TILES):
                result(m)

        @block2.tensor
        def _(pe):
            def norm_transposes(t):
                pe.wait_ge(n2_ready, t + 1)
                if t >= 2:
                    pe.wait_ge(t2_done, t - 1)
                bank = xt_ps[:, t % 2].rearrange("p a n -> p (a n)")
                for c in range(DC):
                    last = nc.tensor.transpose(bank[:, c * P:(c + 1) * P], xg[:, t % 2, c * P:(c + 1) * P], ident[:])
                last.then_inc(t2_ready, 1)

            def gates(t):
                pe.wait_ge(t2_done, t + 1)
                place = (s_sb, g_sb)[t % 2]
                at = z_ps[:, 0].rearrange("p a n -> p (a n)")[:, t * ER:(t + 1) * ER]
                for c in range(DC):
                    last = nc.tensor.matmul(at, place[:, c, 0:P], wr[:, c, :], start=(c == 0), stop=(c == DC - 1))
                last.then_inc(gate_part, 1)

            pe.wait_ge(r_loaded, 48)
            for t in range(TILES):
                norm_transposes(t)
                if t:
                    gates(t - 1)
            gates(TILES - 1)

            def three(out_ps, stat, mov, first, last):
                for a, b in ((0, 0), (0, 1), (1, 0)):
                    ins = nc.tensor.matmul(out_ps, stat[a], mov[b], start=(first and a + b == 0),
                                           stop=(last and a == 1), skip_group_check=True)
                return ins

            def x_transposes(n):
                pe.wait_ge(xg_loaded, n * 32 + 32)
                for b in range(2):
                    for a in range(2):
                        c = 2 * b + a
                        for h in range(2):
                            last = nc.tensor.transpose(xt_ps[:, b, a, h * P:(h + 1) * P],
                                                       xg[:, h, c * P:(c + 1) * P], ident[:])
                    last.then_inc(xt_ready, 1)

            def prefixes():
                pe.wait_ge(picked_ready, 1)
                pe.wait_ge(before_set, 2)
                v = picked[:].rearrange("p t e -> p (t e)")
                at = xt_ps[:, 0].rearrange("p a n -> p (a n)")
                nc.tensor.matmul(at[:, 0:TILES * ER], before[:], v, start=True, stop=True)
                nc.tensor.matmul(at[:, TILES * ER:2 * TILES * ER], ones[:], v, start=True, stop=True)\
                  .then_inc(window_ready, 1)

            def table_part(w):
                pe.wait_ge(hots_ready, w + 1)
                at = xt_ps[:, 0].rearrange("p a n -> p (a n)")[:, 0:COLS]
                for i in range(PART):
                    last = nc.tensor.matmul(at, hot_row[:, i, :], hot_col[:, i, :], start=(i == 0),
                                            stop=(i == PART - 1))
                last.then_inc(window_ready, 1)

            def tile(n, par, window=None, more=True):
                w = w_sb[:, par]
                known = isinstance(n, int)
                pe.wait_ge(xl_done, n * 2 + 2)
                if window is not None:
                    prefixes() if window == 0 else table_part(window - 1)
                for b in range(2):
                    if not known or n:
                        pe.wait_ge(g_done, n * 4 + (2 * b - 2))
                    for c in range(DC):
                        for a in range(2):
                            cols = slice((2 * b + a) * P, (2 * b + a + 1) * P)
                            last = three(u_ps[:, b, a, :], (w[:, 0, 0, c, cols], w[:, 1, 0, c, cols]),
                                         (x_hi[:, c, :], x_lo[:, c, :]), c == 0 and a == 0, c == DC - 1)
                    last.then_inc(u_ready, 1)
                if more:
                    if window is not None:
                        pe.wait_ge(window_read, window + 1)
                    x_transposes(n + 1)
                for b in range(2):
                    if not known or n:
                        pe.wait_ge(s_done, n * 4 + (2 * b - 2))
                    else:
                        pe.wait_ge(sel_ready, 1)
                    for c in range(DC):
                        if b == 0:
                            pe.wait_ge(ul_done, n * 4 + (c + 1))
                        for a in range(2):
                            cols = slice((2 * b + a) * P, (2 * b + a + 1) * P)
                            last = three(z_ps[:, b, a, :], (w[:, 0, 1, c, cols], w[:, 1, 1, c, cols]),
                                         (u_hi[:, c, :], u_lo[:, c, :]), c == 0 and a == 0, c == DC - 1)
                    last.then_inc(z_ready, 1)
                if not known or n:
                    pe.wait_ge(y_done, n * 2)
                for c in range(DC):
                    if c % 2 == 0:
                        pe.wait_ge(gl_done, n * 2 + (c // 2 + 1))
                    for h in range(2):
                        rows = slice(h * P, (h + 1) * P)
                        last = three(y_v[:, h, :], (g_hi[:, c, rows], g_lo[:, c, rows]),
                                     (w[:, 0, 2, c, :], w[:, 1, 2, c, :]), c == 0, c == DC - 1)
                        if c == DC - 1:
                            last.then_inc(y_ready, 1)

            x_transposes(0)
            pe.wait_ge(lo_done, 3)
            for n in range(NA):
                tile(n, 0, window=n - 1 if n in (1,) else {3: 1, 4: 2}.get(n))

            def head(j, par, nth, first):
                pe.wait_ge(lo_done, j * 3 + 3)
                pe.sem_inc(passed)
            total = routed(pe, head, tile)
            pe.wait_ge(lo_done, 3 * (ER + 2))
            for jj in range(NB):
                tile(total + (NA + jj), 0, more=jj < NB - 1)

        @block2.scalar
        def _(act):
            def split(j, par, first=None):
                if first is not None:
                    act.wait_ge(y_ready, first * 2)
                for m in range(3):
                    act.wait_ge(raw_loaded[m], weight_parts(j))
                    nc.scalar.activation(w_sb[:, par, 0, m], w_raw[:, m], ACT.Copy).then_inc(hi_done, 1)

            def x_high(n):
                for b in range(2):
                    act.wait_ge(xt_ready, n * 2 + (b + 1))
                    nc.scalar.activation(x_hi[:, 2 * b:2 * b + 2, :], xt_ps[:, b], ACT.Copy).then_inc(xh_done, 1)

            def tile(n, par, more=True):
                for b in range(2):
                    act.wait_ge(u_ready, n * 2 + (b + 1))
                    for a in range(2):
                        c = 2 * b + a
                        last = nc.scalar.activation(u_hi[:, c, :], u_ps[:, b, a, :], ACT.Identity,
                                                    bias=b_ug[:, par, 0, c:c + 1])
                    last.then_inc(uh_done, 1)
                if more:
                    x_high(n + 1)
                for b in range(2):
                    act.wait_ge(z_ready, n * 2 + (b + 1))
                    if not isinstance(n, int) or n:
                        act.wait_ge(g_done, n * 4)
                    for a in range(2):
                        c = 2 * b + a
                        nc.scalar.activation(s_sb[:, c, :], z_ps[:, b, a, :], ACT.Silu,
                                             bias=b_ug[:, par, 1, c:c + 1]).then_inc(s_done, 1)

            split(0, 0)
            act.wait_ge(sel_ready, 1)
            nc.scalar.activation(prob[:], prob[:], ACT.Exp).then_inc(exp_ready, 1)
            x_high(0)
            split(1, 1)
            act.wait_ge(b_loaded[0], 32)
            for n in range(NA):
                tile(n, 0)

            def head(j, par, nth, first):
                split(j + 1, 1 - par, first)
                act.wait_ge(b_loaded[par], nth * 32 + 32)
            total = routed(act, head, tile)
            act.wait_ge(b_loaded[0], 32 * (ER // 2 + 2))
            for jj in range(NB):
                tile(total + (NA + jj), 0, more=jj < NB - 1)

        @block2.vector
        def _(dve):
            steps = [0]

            def done(ins):
                steps[0] += 1
                ins.then_inc(dve2, 1)
                dve.wait_ge(dve2, steps[0])

            def split(j, par):
                for m in range(3):
                    dve.wait_ge(hi_done, j * 3 + (m + 1))
                    nc.vector.tensor_tensor(w_sb[:, par, 1, m], w_raw[:, m], w_sb[:, par, 0, m].bitcast(FP32),
                                            ALU.subtract).then_inc(lo_done, 1)

            for t in range(TILES):
                done(nc.vector.bn_stats(stats[:], x_sb[:, t, :]))
                done(nc.vector.bn_aggr(mv[:, t, :], stats[:]))
            nc.vector.tensor_scalar(mean_sq[:, 0], mv[:, :, 1], LN_EPS, None, ALU.add).then_inc(var_ready, 1)
            split(0, 0)
            dve.wait_ge(rstd_ready, 1)

            def norm_out(t):
                dve.wait_ge(t2_ready, t + 1)
                if t >= 2:
                    dve.wait_ge(gate_part, t - 1)
                place = (s_sb, g_sb)[t % 2]
                nc.vector.tensor_copy(place[:, :, 0:P], xt_ps[:, t % 2].rearrange("p a (h n) -> p (a h) n", n=P))\
                  .then_inc(t2_done, 1)
            for t in range(TILES):
                if t >= 2:
                    norm_out(t - 2)
                    dve.wait_ge(n2_stored[t % 2], 16 * (t // 2))
                nc.vector.tensor_scalar(xg[:, t % 2, :], x_sb[:, t, :], mv[:, t, 0:1], rsqrt[:, 0, t:t + 1],
                                        ALU.subtract, ALU.mult).then_inc(n2_ready, 1)
            norm_out(TILES - 2)
            norm_out(TILES - 1)

            for e in range(ER):
                nc.vector.memset(order[:, e:e + 1], float(ER - e))
            dve.wait_ge(iota_set, 2)
            nc.vector.tensor_copy(iota_f[:], iota_i[:])
            nc.vector.tensor_copy(token[:], token_i[:])
            dve.wait_ge(r_loaded, 48)
            dve.wait_ge(gate_part, TILES)
            gates = z_ps[:, 0].rearrange("p a n -> p (a n)")[:, 0:TILES * ER].rearrange("p (t e) -> p t e", e=ER)
            done(nc.vector.tensor_tensor(gate[:], gates, brt[:].unsqueeze(1).to_broadcast(whole), ALU.add))
            done(nc.vector.tensor_tensor(biased[:], gate[:], gbt[:].unsqueeze(1).to_broadcast(whole), ALU.add))
            for k in range(2):
                done(nc.vector.tensor_reduce(top[:], biased[:], axis=AX.X, op=ALU.max))
                done(nc.vector.tensor_tensor(key[:], biased[:], top[:].unsqueeze(2).to_broadcast(whole), ALU.is_equal))
                done(nc.vector.tensor_tensor(key[:], key[:], order[:].unsqueeze(1).to_broadcast(whole), ALU.mult))
                done(nc.vector.tensor_reduce(top[:], key[:], axis=AX.X, op=ALU.max))
                done(nc.vector.tensor_tensor(hot[:, k], key[:], top[:].unsqueeze(2).to_broadcast(whole), ALU.is_equal))
                done(nc.vector.tensor_tensor(key[:], hot[:, k], gate[:], ALU.mult))
                done(nc.vector.tensor_reduce(prob[:, k, :], key[:], axis=AX.X, op=ALU.add))
                if k == 0:
                    done(nc.vector.scalar_tensor_tensor(biased[:], hot[:, 0], -3e38, biased[:], ALU.mult, ALU.add))
            nc.vector.tensor_tensor(picked[:], hot[:, 0], hot[:, 1], ALU.add).then_inc(picked_ready, 1)
            done(nc.vector.tensor_tensor(top[:], prob[:, 0, :], prob[:, 1, :], ALU.max))
            both = [P, 2, TILES]
            nc.vector.tensor_tensor(prob[:], prob[:], top[:].unsqueeze(1).to_broadcast(both), ALU.subtract)\
              .then_inc(sel_ready, 1)

            def probabilities():
                dve.wait_ge(exp_ready, 1)
                done(nc.vector.tensor_tensor(top[:], prob[:, 0, :], prob[:, 1, :], ALU.add))
                done(nc.vector.reciprocal(top[:], top[:]))
                done(nc.vector.tensor_tensor(prob[:], prob[:], top[:].unsqueeze(1).to_broadcast(both), ALU.mult))

            def prefixes_out():
                dve.wait_ge(window_ready, 1)
                nc.vector.tensor_copy(prefix[:], xt_ps[:, 0].rearrange("p a n -> p (a n)")[:, 0:2 * TILES * ER]
                                      .rearrange("p (s t e) -> p s t e", s=2, e=ER)).then_inc(window_read, 1)

            def positions():
                dve.wait_ge(window_read, 1)
                done(nc.vector.memset(counts[:, 0, :], 0.0))
                for t in range(TILES):
                    done(nc.vector.tensor_tensor(counts[:, t + 1, :], counts[:, t, :], prefix[:, 1, t, :], ALU.add))
                done(nc.vector.tensor_scalar(tiles_i[:], counts[:, TILES, :], float(TS - 1), None, ALU.add))
                done(nc.vector.tensor_scalar(tiles_i[:], tiles_i[:], 8, None, ALU.arith_shift_right))
                done(nc.vector.tensor_scalar(tiles_f[:], tiles_i[:], 1.0, None, ALU.max))
                done(nc.vector.memset(start_f[:, 0:1], 0.0))
                for e in range(ER):
                    done(nc.vector.tensor_tensor(start_f[:, e + 1:e + 2], start_f[:, e:e + 1], tiles_f[:, e:e + 1],
                                                 ALU.add))
                nc.vector.tensor_copy(start_i[:], start_f[:]).then_inc(start_ready, 1)
                done(nc.vector.tensor_tensor(prefix[:, 0], prefix[:, 0], counts[:, 0:TILES, :], ALU.add))
                done(nc.vector.scalar_tensor_tensor(prefix[:, 0], start_f[:, 0:ER].unsqueeze(1).to_broadcast(whole),
                                                    float(TS), prefix[:, 0], ALU.mult, ALU.add))
                for k in range(2):
                    done(nc.vector.tensor_tensor(key[:], hot[:, k], prefix[:, 0], ALU.mult))
                    done(nc.vector.tensor_reduce(pos_f[:, k, :], key[:], axis=AX.X, op=ALU.add))
                done(nc.vector.tensor_scalar(top[:, 0:1], start_f[:, ER:], float(TS), float(-TS * NA), ALU.mult, ALU.add))
                done(nc.vector.tensor_scalar(pos_f[:, 2, :], token[:], top[:, 0:1], None, ALU.add))
                done(nc.vector.tensor_copy(pos_i[:], pos_f[:]))
                done(nc.vector.tensor_scalar(col_i[:], pos_i[:], 7, None, ALU.arith_shift_right))
                done(nc.vector.tensor_copy(col_f[:], col_i[:]))
                done(nc.vector.scalar_tensor_tensor(row_f[:], col_f[:], float(-P), pos_f[:], ALU.mult, ALU.add))

            def hots(w):
                for i, (k, t) in enumerate(LISTED[w * PART:(w + 1) * PART]):
                    nc.vector.tensor_scalar(hot_row[:, i, :], iota_f[:], row_f[:, k, t:t + 1], None, ALU.is_equal)
                    last = nc.vector.tensor_scalar(hot_col[:, i, :], iota_f[:, 0:COLS], col_f[:, k, t:t + 1],
                                                   token[:, t:t + 1], ALU.is_equal, ALU.mult)
                last.then_inc(hots_ready, 1)

            def table_out(w):
                dve.wait_ge(window_ready, w + 2)
                part = xt_ps[:, 0].rearrange("p a n -> p (a n)")[:, 0:COLS]
                if w == 0:
                    nc.vector.tensor_copy(table_f[:], part).then_inc(window_read, 1)
                else:
                    nc.vector.tensor_tensor(table[:], table_f[:], part, ALU.add).then_inc(window_read, 1)
                    dve.wait_ge(window_read, w + 2)
                    nc.vector.memset(top[:, 0:1], 0.0).then_inc(table_ready, 1)

            def x_low(n):
                for b in range(2):
                    dve.wait_ge(xh_done, n * 2 + (b + 1))
                    two = slice(2 * b, 2 * b + 2)
                    nc.vector.tensor_tensor(x_lo[:, two, :], xt_ps[:, b], x_hi[:, two, :].bitcast(FP32), ALU.subtract)\
                      .then_inc(xl_done, 1)

            def tile(n, par, more=True, x_tile=None):
                bias = b_ug[:, par, 0]
                for b in range(2):
                    dve.wait_ge(uh_done, n * 2 + (b + 1))
                    for a in range(2):
                        c = 2 * b + a
                        nc.vector.scalar_tensor_tensor(u_lo[:, c, :], u_ps[:, b, a, :], bias[:, c:c + 1],
                                                       u_hi[:, c, :].bitcast(FP32), ALU.add, ALU.subtract)\
                          .then_inc(ul_done, 1)
                if more:
                    x_low(n + 1)
                for b in range(2):
                    dve.wait_ge(s_done, n * 4 + (2 * b + 2))
                    for a in range(2):
                        c = 2 * b + a
                        nc.vector.scalar_tensor_tensor(g_sb[:, c, :], u_ps[:, b, a, :], bias[:, c:c + 1],
                                                       s_sb[:, c, :], ALU.add, ALU.mult).then_inc(g_done, 1)
                    two = slice(2 * b, 2 * b + 2)
                    dve.wait_ge(g_done, n * 4 + (2 * b + 2))
                    nc.vector.tensor_copy(g_hi[:, two, :], g_sb[:, two, :]).then_inc(gh_done, 1)
                    dve.wait_ge(gh_done, n * 2 + (b + 1))
                    nc.vector.tensor_tensor(g_lo[:, two, :], g_sb[:, two, :], g_hi[:, two, :].bitcast(FP32),
                                            ALU.subtract).then_inc(gl_done, 1)
                for h in range(2):
                    dve.wait_ge(y_ready, n * 2 + (h + 1))
                    if x_tile is None and h == 0:
                        dve.wait_ge(y_stored, (n - NA) * 32)
                    nc.vector.tensor_tensor(y_sb[:, h, :], y_v[:, h, :], bd[:, par, :], ALU.add).then_inc(y_done, 1)
                    if x_tile is not None:
                        dve.wait_ge(y_done, n * 2 + (h + 1))
                        at = x_sb[:, x_tile + h, :]
                        nc.vector.tensor_tensor(at, at, y_sb[:, h, :], ALU.add)

            x_low(0)
            split(1, 1)
            dve.wait_ge(b_loaded[0], 32)
            tile(0, 0, x_tile=0)
            prefixes_out()
            probabilities()
            tile(1, 0, x_tile=2)
            positions()
            tile(2, 0, x_tile=4)
            hots(0)
            table_out(0)
            tile(3, 0, x_tile=6)
            hots(1)
            table_out(1)
            tile(4, 0, x_tile=8)

            def head(j, par, nth, first):
                split(j + 1, 1 - par)
                dve.wait_ge(b_loaded[par], nth * 32 + 32)
                dve.sem_inc(passed)
            total = routed(dve, head, tile)
            dve.wait_ge(b_loaded[0], 32 * (ER // 2 + 2))
            dve.wait_ge(y_stored, total * 32)

            def add(t):
                for k in range(2):
                    m = 2 * t + k
                    dve.wait_ge(yg_loaded[m % RING], 16 * (m // RING + 1))
                    if k:
                        dve.wait_ge(added, m)
                    nc.vector.scalar_tensor_tensor(x_sb[:, t, :], yg[:, m % RING, :], prob[:, k, t:t + 1], x_sb[:, t, :],
                                                   ALU.mult, ALU.add).then_inc(added, 1)
            for jj in range(NB):
                tile(total + (NA + jj), 0, more=jj < NB - 1, x_tile=2 * (NA + jj))
                for t in range(5 * jj, 5 * jj + 5 if jj < NB - 1 else TILES):
                    add(t)


def kernel(**inputs):
    import numpy as np
    import concourse.bacc as bacc
    from concourse.bass_utils import run_bass_kernel_spmd

    nc = bacc.Bacc("TRN2", target_bir_lowering=False, num_devices=1, dynamic_dma_scratch_size=8192)
    a = {k.replace("L0_", ""): np.asarray(v) for k, v in inputs.items()}
    x, context = a["x"], a["ctx_2048"]
    d = x.shape[-1]
    kv = np.concatenate([a["xattn_Wk"], a["xattn_Wv"]], axis=0)
    wk, wv = kv[0::2].T.reshape(d, -1, 1, P), kv[1::2].T.reshape(d, -1, 1, P)
    f = {n: a["ffn_" + n] for n in ("Wr", "br", "gate_bias", "Wup", "bup", "Wgate", "bgate", "Wdown", "bdown",
                                    "Wsu", "bsu", "Wsg", "bsg", "Wsd", "bsd")}
    w = np.stack([np.concatenate([f[s][None], f[r], f[s][None]]) for r, s in (
        ("Wup", "Wsu"), ("Wgate", "Wsg"), ("Wdown", "Wsd"))], axis=1)
    b = np.stack([np.concatenate([f[s][None], f[r], f[s][None]]) for r, s in (("bup", "bsu"), ("bgate", "bsg"))],
                 axis=1)
    arrays = {
        "x": x.reshape(-1, d),
        "ctx_t": context.transpose(0, 2, 1),
        "wq_t": a["xattn_Wq"].T,
        "wkv_t": np.concatenate([wk, wv], axis=2).reshape(d, -1),
        "w_all": w.reshape(w.shape[0], 3, d // P, P, d).transpose(0, 3, 1, 2, 4),
        "b_up_gate": b.reshape(b.shape[0], 2, d // P, P).transpose(0, 3, 1, 2),
        "b_down": np.concatenate([f["bsd"][None], f["bdown"], f["bsd"][None]]),
        "w_router": f["Wr"].reshape(d // P, P, -1).transpose(1, 0, 2),
        "b_router": f["br"],
        "gate_bias": f["gate_bias"],
    }
    arrays = {k: np.ascontiguousarray(v) for k, v in arrays.items()}
    args = [nc.dram_tensor(k, v.shape, mybir.dt.from_np(v.dtype), kind="ExternalInput").ap()
            for k, v in arrays.items()]
    n = arrays["x"].shape[0]
    args.append(nc.dram_tensor("xn_dram", (n, d), FP32, kind="Internal").ap())
    args.append(nc.dram_tensor("y_dram", (2 * n + 2 * P * f["Wr"].shape[1], d), FP32, kind="Internal").ap())
    out = nc.dram_tensor("out", arrays["x"].shape, FP32, kind="ExternalOutput").ap()
    moe_layer(nc, *args, out)
    r = run_bass_kernel_spmd(nc, [arrays], core_ids=[0])
    return r.results[0]["out"].reshape(x.shape)
```

```python
from contextlib import ExitStack

import concourse.bass as bass
from concourse import mybir

FP32 = mybir.dt.float32
FP32R = mybir.dt.float32r
ALU = mybir.AluOpType
ACT = mybir.ActivationFunctionType
AX = mybir.AxisListType

P = 128


class Tally:

    def __init__(self, sem):
        self.sem, self.const, self.turns = sem, 0, 0

    def next(self, by=1):
        self.const += by
        return self.now()

    def now(self, less=0):
        return self.turns + (self.const - less)

    def past(self, n):
        return not isinstance(self.turns, int) or self.const > n


def moe_layer(nc, x, ctx_t, wq_t, wkv_t, w_all, b_up_gate, b_down, w_router, b_router, gate_bias, xn_dram, y_dram,
              out):
    TOKENS, D = x.shape
    BATCH = ctx_t.shape[0]
    SEQ = TOKENS // BATCH
    CTX = ctx_t.shape[2]
    DC = D // P
    HD = 16
    TILES = TOKENS // P
    BT = SEQ // P
    MT = CTX // P
    GROUPS = DC
    GH = P // HD
    PAIRS = GH // 2
    ER = w_router.shape[2]
    LN_EPS, RMS_EPS = 1e-5, 1e-6

    with ExitStack() as ctx:
        att = ExitStack()
        def sb(name, shape, dt=FP32):
            return ctx.enter_context(nc.sbuf_tensor(name, shape, dt))

        def ps(name, shape):
            return att.enter_context(nc.psum_tensor(name, shape, FP32))

        def sem(name):
            return ctx.enter_context(nc.semaphore(name))

        x_sb = sb("x_sb", [P, TILES, D])
        ident = sb("ident", [P, P])
        ident_r = sb("ident_r", [P, P], FP32R)
        w_raw = sb("w_raw", [P, 3, DC, D])
        raw_loaded = [sem(f"raw_loaded{m}") for m in range(3)]
        stats = sb("stats", [P, 6])
        power = sb("power", [P, 2 * 8])
        mean_sq = sb("mean_sq", [P, 3, 2 * 8])
        rsqrt = sb("rsqrt", [P, 3, 2 * 8])

        gate = sb("gate", [P, TILES, ER])
        wr = sb("wr", [P, DC, ER])
        brt, gbt = sb("brt", [P, ER]), sb("gbt", [P, ER])
        mv2 = sb("mv2", [P, BT, 2])

        def asb(name, shape, dt=FP32):
            return att.enter_context(nc.sbuf_tensor(name, shape, dt))

        mv = asb("mv", [P, TILES, 2])
        rstd = asb("rstd", [P, TILES])
        wq = asb("wq", [P, DC, D])
        wkv = w_raw[:, 1:].rearrange("p m c n -> p (m c n)").rearrange("p (c g n) -> p c g n", c=DC, n=2 * P)
        wkv_hi, wkv_lo = (asb(n, [P, DC, GROUPS, 2 * P], FP32R) for n in ("wkv_hi", "wkv_lo"))
        ctx_sb = asb("ctx_sb", [P, DC, CTX])
        ctx_hi, ctx_lo = (asb(n, [P, DC, CTX], FP32R) for n in ("ctx_hi", "ctx_lo"))
        xn_t = asb("xn_t", [P, DC, SEQ])
        xn = asb("xn", [P, 2, D])
        raw = asb("raw", [P, 2, 2 * GH, HD])
        sq = asb("sq", [P, 2 * GH, HD])
        qn = asb("qn", [P, 2, 2 * GH, HD])
        split = asb("split", [P, 2, 2, GH, 4, HD])
        q_stack = asb("q_stack", [P, 2, PAIRS, SEQ], FP32R)
        k_stack = asb("k_stack", [P, 2, PAIRS, CTX], FP32R)
        v_sb = asb("v_sb", [P, 2, MT, GH, 2 * HD])
        probs = asb("probs", [P, 2, 4, SEQ])
        o_sb = asb("o_sb", [P, SEQ])
        o_n = asb("o_n", [P, BT, 4, HD])
        rec = asb("rec", [P, BT, 4])
        xt2 = asb("xt2", [P, 2, DC, P])
        zeros = asb("zeros", [P, 1, D])

        scores = ps("scores", [P, 2, 2, SEQ])
        o_ps = ps("o_ps", [P, SEQ])
        pj = ps("pj", [P, 512])
        tr = ps("tr", [P, 2, 512])

        w_first, w_rest = sem("w_first"), sem("w_rest")
        r_loaded = sem("r_loaded")
        n2_ready = sem("n2_ready")
        n2_stored = [sem("n2_stored0"), sem("n2_stored1")]
        x_first = sem("x_first")
        x_rest = sem("x_rest")
        ctx_loaded = sem("ctx_loaded")
        high_done, wkv_split, ctx_split = sem("high_done"), sem("wkv_split"), sem("ctx_split")
        ones_set = sem("ones_set")
        ident_zero = sem("ident_zero")
        zeros_set, y_filled = sem("zeros_set"), sem("y_filled")
        ident_set = sem("ident_set")
        xn_ready = sem("xn_ready")
        tr_ready = sem("tr_ready")
        tr_free = sem("tr_free")
        k_free = sem("k_free")
        pj_ready = sem("pj_ready")
        pj_free = sem("pj_free")
        split_ready = sem("split_ready")
        sc_ready = sem("sc_ready")
        p_ready = sem("p_ready")
        pv_done = sem("pv_done")
        o_evac = sem("o_evac")
        dve_step = sem("dve_step")
        mean_ready = sem("mean_ready")
        power_set = sem("power_set")
        rsqrt_ready = sem("rsqrt_ready")

        passed = sem("passed")

        block = att.enter_context(nc.Block())

        def bcast(v, n):
            return v.rearrange("(a n) -> a n", a=1).to_broadcast([P, n])

        def loop_over_batches(engine, tallies, turn):
            with engine.Fori(1, BATCH) as r:
                before = [t.const for t in tallies]
                per_turn = [TURN[t.sem.name] for t in tallies]
                for t, n in zip(tallies, per_turn):
                    t.turns = (r - 1) * n
                turn(r)
            for t, n, was in zip(tallies, per_turn, before):
                assert t.const - was == n, (t.sem.name, t.const - was)
                t.turns = 0
                t.const += n * (BATCH - 2)

        transposed = BT + 4 * (2 * BT + 2) + 2 * BT
        k_stacks = 4 * BT
        TURN = {"xn_ready": BT, "n2_ready": BT, "tr_ready": transposed, "tr_free": transposed - k_stacks,
                "k_free": k_stacks,
                "pj_ready": 4 * BT, "pj_free": 4 * BT, "split_ready": 4 * BT, "sc_ready": 4 * 16,
                "p_ready": 4 * 16, "pv_done": 4 * 8, "o_evac": 8,
                "dve_step": 8 * 2 + 16 * 5 + 2 * BT + BT,
                "rsqrt_ready": 4 * BT + 1}

        PROJECTIONS = {0: 0, 1: 1, 2: 2, 3: 3}
        SPLITS = {2: 0, 3: 1, 5: 3}
        LATE_SPLITS = {3: 2}
        STACKS = {3: 0, 4: 1, 5: 2, 6: 3}

        ROUTER_STEP = 8 + 7

        def bank_order(k, s, first=False, last=False, ln2=None):
            new_batch, i = k == GROUPS - 1 and not last, 8 * k + s - ROUTER_STEP
            return (["x", "x"] * (new_batch and s == 0) + ["q", "k"] * (not last and s in STACKS)
                    + ["x"] * (new_batch and s + 2 < BT) + ["out"] * (s == 5 or (s == 1 and not first))
                    + ["x2"] * (ln2 is not None and 0 <= i < BT) + ["gates"] * (ln2 is not None and 0 < i <= BT))


        @block.gpsimd
        def _(pool):
            nc.gpsimd.memset(ident[:], 0.0).then_inc(ident_zero, 1)
            nc.gpsimd.memset(zeros[:], 0.0).then_inc(zeros_set, 1)
            nc.gpsimd.memset(v_sb[:, :, :, :, HD:], 1.0).then_inc(ones_set, 1)
            pool.wait_ge(ident_zero, 1)
            nc.gpsimd.affine_select(out=ident[:], in_=ident[:], compare_op=ALU.not_equal, fill=1.0, base=0,
                                    pattern=[[-1, P]], channel_multiplier=1).then_inc(ident_set, 1)
            pool.wait_ge(ident_set, 1)
            nc.gpsimd.tensor_copy(ident_r[:], ident[:]).then_inc(ident_set, 1)
            nc.gpsimd.memset(power[:], -0.5).then_inc(power_set, 1)
            pool.wait_ge(power_set, 1)

            def root(n, half, width=2 * GH):
                pool.wait_ge(mean_ready, n + 1)
                nc.gpsimd.tensor_tensor(rsqrt[:, half, 0:width], mean_sq[:, half, 0:width], power[:, 0:width],
                                        ALU.pow).then_inc(rsqrt_ready, 1)
            root(0, 0, BT)
            with pool.Fori(0, GROUPS * BT // 2) as i:
                root(i * 2 + 1, 0)
                root(i * 2 + 2, 1)
            root(GROUPS * BT + 1, 0, TILES - BT)
            per_turn = GROUPS * BT + 1
            with pool.Fori(0, BATCH - 1) as r:
                for n in range(per_turn):
                    at = r * per_turn + (GROUPS * BT + 2 + n)
                    if n < 2 * BT:
                        root(at, n % 2)
                    elif n == 2 * BT:
                        root(at, 2, BT)
                    else:
                        root(at, (n - 1) % 2)

        @block.sync
        def _(sp):
            x_v = x.rearrange("(t p) d -> p t d", p=P)
            sp.dma_start(x_sb[:, 0:BT, :], x_v[:, 0:BT, :]).then_inc(x_first, 16)
            wq_v = wq_t.rearrange("(c p) n -> p c n", p=P)
            wkv_v = wkv_t.rearrange("(c p) (g n) -> p c g n", p=P, n=2 * P)
            sp.dma_start(wq[:, :, 0:P], wq_v[:, :, 0:P]).then_inc(w_first, 16)
            sp.dma_start(wkv[:, :, 0], wkv_v[:, :, 0]).then_inc(w_first, 16)
            sp.dma_start(ctx_sb[:], ctx_t[0, :, :].rearrange("(c p) m -> p c m", p=P)).then_inc(ctx_loaded, 16)
            sp.dma_start(wq[:, :, P:], wq_v[:, :, P:]).then_inc(w_rest, 16)
            sp.dma_start(wkv[:, :, 1:], wkv_v[:, :, 1:]).then_inc(w_rest, 16)
            sp.dma_start(wr[:], w_router).then_inc(r_loaded, 16)
            sp.dma_start(brt[:], bcast(b_router, ER)).then_inc(r_loaded, 16)
            sp.dma_start(gbt[:], bcast(gate_bias, ER)).then_inc(r_loaded, 16)
            sp.dma_start(x_sb[:, BT:, :], x_v[:, BT:, :]).then_inc(x_rest, 16)
            sp.dma_start(w_raw[:, 0], w_all[0, :, 0]).then_inc(raw_loaded[0], 16)
            sp.wait_ge(zeros_set, 1)
            fill = y_dram[2 * TOKENS:, :].rearrange("(s p) d -> p s d", p=P)
            sp.dma_start(fill, zeros[:].to_broadcast([P, fill.shape[1], D])).then_inc(y_filled, 16)
            sp.wait_ge(wkv_split, GROUPS)
            for m in range(1, 3):
                sp.dma_start(w_raw[:, m], w_all[0, :, m]).then_inc(raw_loaded[m], 16)
            with sp.Fori(1, BATCH) as b:
                sp.wait_ge(ctx_split, b * BT)
                sp.dma_start(ctx_sb[:], ctx_t[bass.ds(b, 1), :, :].rearrange("a (c p) m -> p (a c) m", p=P))\
                  .then_inc(ctx_loaded, 16)
                for t in range(BT):
                    sp.wait_ge(n2_ready, (b - 1) * BT + (t + 1))
                    sp.dma_start(xn_dram.rearrange("(t p) d -> p t d", p=P)[:, bass.ds((b - 1) * BT + t, 1), :],
                                 xn[:, t % 2:t % 2 + 1, :]).then_inc(n2_stored[t % 2], 16)
            sp.wait_ge(y_filled, 16)
            for par in range(2):
                sp.wait_ge(n2_stored[par], 16 * (TILES - BT) // 2)

        @block.tensor
        def _(pe):
            xn_r, trr, trf, kf = Tally(xn_ready), Tally(tr_ready), Tally(tr_free), Tally(k_free)
            pjr, spl = Tally(pj_ready), Tally(split_ready)
            scr, pvd, orr = Tally(sc_ready), Tally(pv_done), Tally(o_evac)
            n2r = Tally(n2_ready)
            tallies = [xn_r, trr, trf, kf, pjr, spl, scr, pvd, orr, n2r]
            readers = []

            in_xn_t, in_xt2 = {}, {}

            def take_bank(reader):
                if len(readers) >= 2:
                    before = readers[-2]
                    pe.wait_ge(before.sem, before.now(int(readers[-1] is before)))
                readers.append(reader)
                reader.next()
                trr.next()

            def transposes(sources, rounded=False, reader=None):
                take_bank(reader or trf)
                for i, src in enumerate(sources):
                    at = tr[:, trr.const % 2, i * P:(i + 1) * P]
                    if rounded:
                        last = nc.tensor.transpose(at.bitcast(FP32R), src.bitcast(FP32R), ident_r[:])
                    else:
                        last = nc.tensor.transpose(at, src, ident[:])
                last.then_inc(tr_ready, 1)

            def norm_transposes(t):
                pe.wait_ge(xn_ready, xn_r.next())
                transposes([xn[:, t % 2, c * P:(c + 1) * P] for c in range(DC)])
                in_xn_t[t] = trf.now()

            def project(g, t, batch):
                if batch is not None:
                    pe.wait_ge(ctx_split, batch * BT + (t + 1))
                    pe.wait_ge(tr_free, in_xn_t[t])
                pjr.next()
                if pjr.past(1):
                    pe.wait_ge(pj_free, pjr.now(1))
                for c in range(DC):
                    nc.tensor.matmul(pj[:, 0:P], xn_t[:, c, t * P:(t + 1) * P], wq[:, c, g * P:(g + 1) * P],
                                     start=(c == 0), stop=(c == DC - 1))
                for c in range(DC):
                    for rows, w in ((ctx_hi, wkv_hi), (ctx_hi, wkv_lo), (ctx_lo, wkv_hi)):
                        last = nc.tensor.matmul(pj[:, P:3 * P], rows[:, c, t * P:(t + 1) * P], w[:, c, g, :],
                                                start=(c == 0 and rows is ctx_hi and w is wkv_hi),
                                                stop=(c == DC - 1 and rows is ctx_lo))
                last.then_inc(pj_ready, 1)

            def stack_transposes(t):
                pe.wait_ge(split_ready, spl.next())
                for qk in range(2):
                    rows = split[:, t % 2, qk].rearrange("p h s d -> p (h s d)")
                    transposes([rows[:, i * P:(i + 1) * P] for i in range(PAIRS)], rounded=True,
                               reader=kf if qk else trf)

            def score(par, s):
                g4, mt = divmod(s, MT)
                for a in range(2):
                    scr.next()
                    if scr.past(2):
                        pe.wait_ge(p_ready, scr.now(2))
                    hp = g4 * 2 + a
                    for i in range(2):
                        rows = slice(64 * i, 64 * i + 64)
                        last = nc.tensor.matmul(scores[:, a, i, :], k_stack[rows, par, hp, mt * P:(mt + 1) * P],
                                                q_stack[rows, par, hp, :], start=True, stop=True)
                    last.then_inc(sc_ready, 1)

            def weigh(par, s, behind):
                g4, mt = divmod(s, MT)
                pe.wait_ge(p_ready, scr.now(behind))
                if mt == 0:
                    if orr.past(0):
                        pe.wait_ge(o_evac, orr.now())
                for j in range(4):
                    last = nc.tensor.matmul(o_ps[32 * j:32 * j + 32, :], v_sb[:, par, mt, 4 * g4 + j, :],
                                            probs[:, s % 2, j, :], start=(mt == 0), stop=(mt == MT - 1))
                pvd.next()
                last.then_inc(pv_done, 1)
                if mt == MT - 1:
                    orr.next()

            def out_transposes():
                pe.wait_ge(o_evac, orr.now())
                transposes([o_sb[:, t * P:(t + 1) * P] for t in range(BT)])

            def norm2_transposes(i):
                pe.wait_ge(n2_ready, n2r.next())
                transposes([xn[:, i % 2, c * P:(c + 1) * P] for c in range(DC)])
                in_xt2[i] = trf.now()

            def gates(i):
                take_bank(trf)
                pe.wait_ge(tr_free, in_xt2[i])
                for c in range(DC):
                    last = nc.tensor.matmul(tr[:, trr.const % 2, 0:ER], xt2[:, i % 2, c, :], wr[:, c, :],
                                            start=(c == 0), stop=(c == DC - 1))
                last.then_inc(tr_ready, 1)

            def unit(k, batch, first=False, last=False, ln2=None):
                par, nxt = k % 2, (k + 1) % GROUPS
                new_batch = k == GROUPS - 1 and not last
                for s in range(8):
                    if s == 0:
                        pe.wait_ge(tr_free, trf.now())
                        pe.wait_ge(k_free, kf.now())
                    score(par, s)
                    if new_batch and s == 0:
                        norm_transposes(0)
                        norm_transposes(1)
                    if not last and s in STACKS:
                        stack_transposes(STACKS[s])
                    if first and s == 0:
                        pe.wait_ge(wkv_split, 2)
                    if not last and s in PROJECTIONS:
                        project(nxt, PROJECTIONS[s], batch + 1 if new_batch else None)
                    if s:
                        weigh(par, s - 1, 2)
                    elif not first:
                        weigh(1 - par, 7, 2)
                    if new_batch and s + 2 < BT:
                        norm_transposes(s + 2)
                    if s == 5 or (s == 1 and not first):
                        out_transposes()
                    i = 8 * k + s - ROUTER_STEP
                    if ln2 is not None and 0 <= i < BT:
                        norm2_transposes(i)
                    if ln2 is not None and 0 < i <= BT:
                        gates(i - 1)

            pe.wait_ge(ident_set, 2)
            pe.wait_ge(ones_set, 1)
            norm_transposes(0)
            norm_transposes(1)
            pe.wait_ge(w_first, 32)
            pe.wait_ge(wkv_split, 1)
            project(0, 0, 0)
            norm_transposes(2)
            norm_transposes(3)
            project(0, 1, 0)
            project(0, 2, 0)
            stack_transposes(0)
            project(0, 3, 0)
            for t in range(1, BT):
                stack_transposes(t)
            pe.wait_ge(w_rest, 32)
            unit(0, 0, first=True)
            pe.wait_ge(wkv_split, GROUPS)
            unit(1, 0)
            unit(2, 0)
            pe.wait_ge(r_loaded, 48)

            def turn(r):
                unit(3, r - 1)
                for k in range(3):
                    unit(k, r, ln2=r - 1)
            loop_over_batches(pe, tallies, turn)
            unit(3, BATCH - 1, last=True)
            weigh(1, 7, 0)
            out_transposes()

        @block.scalar
        def _(act):
            scr, steps, trr = Tally(sc_ready), Tally(pv_done), Tally(tr_ready)

            def group_out():
                act.wait_ge(pv_done, steps.now())
                nc.scalar.copy(o_sb[:], o_ps[:]).then_inc(o_evac, 1)

            def k_stack_out(par, t):
                act.wait_ge(tr_ready, trr.now())
                src = tr[:, trr.const % 2, :].rearrange("p (a b) -> p a b", b=P)
                nc.scalar.copy(k_stack[:, par, :, t * P:(t + 1) * P], src).then_inc(k_free, 1)

            def unit(k, first=False, last=False, ln2=None):
                for s in range(8):
                    for a in range(2):
                        act.wait_ge(sc_ready, scr.next())
                        if a == 0 and steps.past(1):
                            act.wait_ge(pv_done, steps.now(1))
                        nc.scalar.activation(probs[:, s % 2, 2 * a:2 * a + 2, :], scores[:, a], ACT.Exp,
                                             scale=float(HD) ** 0.5).then_inc(p_ready, 1)
                    for what in bank_order(k, s, first, last, ln2):
                        trr.next()
                        if what == "k":
                            k_stack_out(1 - k % 2, STACKS[s])
                    if s == 4 or (s == 0 and not first):
                        group_out()
                    steps.next()

            act.wait_ge(w_first, 32)
            nc.scalar.copy(wkv_hi[:, :, 0], wkv[:, :, 0]).then_inc(high_done, 1)
            act.wait_ge(ctx_loaded, 16)
            nc.scalar.copy(ctx_hi[:], ctx_sb[:]).then_inc(high_done, 1)
            act.wait_ge(w_rest, 32)
            for g in range(1, GROUPS):
                nc.scalar.copy(wkv_hi[:, :, g], wkv[:, :, g]).then_inc(high_done, 1)
            trr.next(BT)
            for t in range(BT):
                trr.next(2)
                k_stack_out(0, t)
            for k in range(3):
                unit(k, first=(k == 0))

            def turn(r):
                unit(3)
                for k in range(3):
                    unit(k, ln2=r - 1)
            loop_over_batches(act, [scr, steps, trr], turn)
            unit(3, last=True)
            group_out()

        @block.vector
        def _(dve):
            trr, trf, pjr, step = Tally(tr_ready), Tally(tr_free), Tally(pj_ready), Tally(dve_step)
            rsq = Tally(rsqrt_ready)
            tallies = [trr, trf, pjr, step, rsq]

            def done(ins):
                ins.then_inc(dve_step, 1)
                dve.wait_ge(dve_step, step.next())

            def root():
                dve.wait_ge(rsqrt_ready, rsq.next())

            def stat(t):
                done(nc.vector.bn_stats(stats[:], x_sb[:, t, :]))
                done(nc.vector.bn_aggr(mv[:, t, :], stats[:]))

            def wkv_low(g):
                dve.wait_ge(high_done, g + 1 if g == 0 else g + 2)
                nc.vector.tensor_tensor(wkv_lo[:, :, g], wkv[:, :, g], wkv_hi[:, :, g].bitcast(FP32), ALU.subtract)\
                  .then_inc(wkv_split, 1)

            def ctx_low(t):
                cols = slice(t * P, (t + 1) * P)
                nc.vector.tensor_tensor(ctx_lo[:, :, cols], ctx_sb[:, :, cols], ctx_hi[:, :, cols].bitcast(FP32),
                                        ALU.subtract).then_inc(ctx_split, 1)

            def split_context(batch, t):
                dve.wait_ge(ctx_loaded, batch * 16 + 16)
                cols = slice(t * P, (t + 1) * P)
                done(nc.vector.tensor_copy(ctx_hi[:, :, cols], ctx_sb[:, :, cols]))
                ctx_low(t)

            def ask_deviations(tiles):
                n = tiles.stop - tiles.start
                nc.vector.tensor_scalar(mean_sq[:, 0, 0:n], mv[:, tiles, 1], LN_EPS, None, ALU.add)\
                  .then_inc(mean_ready, 1)

            def deviations(tiles):
                root()
                done(nc.vector.tensor_copy(rstd[:, tiles], rsqrt[:, 0, 0:tiles.stop - tiles.start]))

            def norm(batch, t):
                tile = batch * BT + t
                nc.vector.tensor_scalar(xn[:, t % 2, :], x_sb[:, tile, :], mv[:, tile, 0:1], rstd[:, tile:tile + 1]
                                        if isinstance(tile, int) else rstd[:, bass.ds(tile, 1)],
                                        ALU.subtract, ALU.mult).then_inc(xn_ready, 1)

            def evacuate(dst):
                dve.wait_ge(tr_ready, trr.next())
                src = tr[:, trr.const % 2, :].rearrange("p (a b) -> p a b", b=P)
                nc.vector.tensor_copy(dst, src).then_inc(tr_free, 1)
                trf.next()

            def norm_out(t):
                evacuate(xn_t[:, :, t * P:(t + 1) * P])

            def project_out(par, t):
                dve.wait_ge(pj_ready, pjr.next())
                done(nc.vector.tensor_copy(raw[:, t % 2], pj[:, 0:2 * P].rearrange("p (h d) -> p h d", d=HD)))
                done(nc.vector.tensor_tensor(sq[:], raw[:, t % 2], raw[:, t % 2], ALU.mult))
                sums = mean_sq[:, t % 2]
                done(nc.vector.tensor_reduce(sums, sq[:], axis=AX.X, op=ALU.add))
                nc.vector.tensor_scalar(sums, sums, HD * RMS_EPS, None, ALU.add).then_inc(mean_ready, 1)
                nc.vector.tensor_copy(v_sb[:, par, t, :, 0:HD], pj[:, 2 * P:3 * P].rearrange(
                    "p (h d) -> p h d", d=HD)).then_inc(pj_free, 1)

            def split_out(t):
                root()
                done(nc.vector.tensor_tensor(qn[:, t % 2], raw[:, t % 2], rsqrt[:, t % 2].unsqueeze(2)
                                             .to_broadcast([P, 2 * GH, HD]), ALU.mult))
                q, k = split[:, t % 2, 0], split[:, t % 2, 1]
                twice = [P, GH, 2, HD]
                q_in = qn[:, t % 2, 0:GH, :].unsqueeze(2).to_broadcast(twice)
                k_in = qn[:, t % 2, GH:, :].unsqueeze(2).to_broadcast(twice)
                nc.vector.tensor_copy(q[:, :, 0:2, :].bitcast(FP32R), q_in)
                done(nc.vector.tensor_copy(k[:, :, 0:4:2, :].bitcast(FP32R), k_in))
                nc.vector.tensor_tensor(q[:, :, 2:4, :].bitcast(FP32R), q_in, q[:, :, 0:2, :], ALU.subtract)
                nc.vector.tensor_tensor(k[:, :, 1:4:2, :].bitcast(FP32R), k_in, k[:, :, 0:4:2, :], ALU.subtract)\
                  .then_inc(split_ready, 1)

            def stacks_out(par, t):
                evacuate(q_stack[:, par, :, t * P:(t + 1) * P])
                trr.next()

            def finalize(batch, g, g4):
                dve.wait_ge(tr_ready, trr.next())
                o_t = tr[:, trr.const % 2, :].rearrange("p (t h d) -> p t h d", t=BT, d=2 * HD)
                done(nc.vector.reciprocal(rec[:], o_t[:, :, :, HD]))
                nc.vector.tensor_tensor(o_n[:], o_t[:, :, :, 0:HD],
                                        rec[:].unsqueeze(3).to_broadcast([P, BT, 4, HD]), ALU.mult)\
                  .then_inc(tr_free, 1)
                dve.wait_ge(tr_free, trf.next())
                cols = g * P + g4 * 4 * HD
                xs = x_sb[:, bass.ds(batch * BT, BT), cols:cols + 4 * HD]
                done(nc.vector.tensor_tensor(xs, xs, o_n[:].rearrange("p t h d -> p t (h d)"), ALU.add))

            def second_norm(k, s, batch):
                if k == 0 and s == 7:
                    for t in range(BT):
                        done(nc.vector.bn_stats(stats[:], x_sb[:, bass.ds(batch * BT + t, 1), :]
                                                .rearrange("p a d -> p (a d)")))
                        dve.sem_inc(passed)
                        done(nc.vector.bn_aggr(mv2[:, t, :], stats[:]))
                if k == 0 and s == 7:
                    nc.vector.tensor_scalar(mean_sq[:, 2, 0:BT], mv2[:, :, 1], LN_EPS, None, ALU.add)\
                      .then_inc(mean_ready, 1)
                if k == 1 and s == 1:
                    root()
                    for t in range(2):
                        norm2(batch, t)
                t = 8 * k + s - ROUTER_STEP
                if 0 <= t < BT:
                    evacuate(xt2[:, t % 2])
                    if t + 2 < BT:
                        dve.wait_ge(n2_stored[t % 2], batch * (16 * BT // 2) + 16)
                        norm2(batch, t + 2)
                if 0 < t <= BT:
                    gates_out(batch, t - 1)

            def norm2(batch, t):
                nc.vector.tensor_scalar(xn[:, t % 2, :], x_sb[:, bass.ds(batch * BT + t, 1), :]
                                        .rearrange("p a d -> p (a d)"), mv2[:, t, 0:1], rsqrt[:, 2, t:t + 1],
                                        ALU.subtract, ALU.mult).then_inc(n2_ready, 1)

            def gates_out(batch, t):
                dve.wait_ge(tr_ready, trr.next())
                nc.vector.tensor_tensor(gate[:, bass.ds(batch * BT + t, 1), :],
                                        tr[:, trr.const % 2, 0:ER].unsqueeze(1), brt[:].unsqueeze(1), ALU.add)\
                  .then_inc(tr_free, 1)
                trf.next()

            def unit(k, batch, first=False, last=False, between=None, ln2=None):
                par = k % 2
                new_batch = k == GROUPS - 1 and not last
                before = (batch, k - 1) if k else (batch - 1, GROUPS - 1)
                for s in range(8):
                    if new_batch and s == 0:
                        if not isinstance(batch, int):
                            for par2 in range(2):
                                dve.wait_ge(n2_stored[par2], batch * (16 * BT // 2))
                        norm(batch + 1, 0)
                        norm(batch + 1, 1)
                    if new_batch and s == 0:
                        split_context(batch + 1, 0)
                        for t in range(2):
                            norm_out(t)
                            norm(batch + 1, t + 2)
                    if not last and s in STACKS:
                        stacks_out(1 - par, STACKS[s])
                    if not last and s in SPLITS:
                        split_out(SPLITS[s])
                    if new_batch and s + 1 < BT:
                        split_context(batch + 1, s + 1)
                    if not last and s in PROJECTIONS:
                        project_out(1 - par, PROJECTIONS[s])
                    if new_batch and s + 2 < BT:
                        norm_out(s + 2)
                    if s == 1 and not first:
                        finalize(*before, 1)
                    if s == 5:
                        finalize(batch, k, 0)
                    if not last and s in LATE_SPLITS:
                        split_out(LATE_SPLITS[s])
                    if ln2 is not None:
                        second_norm(k, s, ln2)
                    if between:
                        between(s)

            nc.vector.memset(mean_sq[:], 1.0)
            dve.wait_ge(x_first, 16)
            for t in range(BT):
                stat(t)
            ask_deviations(slice(0, BT))
            wkv_low(0)
            deviations(slice(0, BT))
            norm(0, 0)
            norm(0, 1)
            dve.wait_ge(high_done, 2)
            ctx_low(0)
            ctx_low(1)
            for t in range(2):
                norm_out(t)
                norm(0, t + 2)
            project_out(0, 0)
            norm_out(2)
            norm_out(3)
            ctx_low(2)
            ctx_low(3)
            project_out(0, 1)
            split_out(0)
            project_out(0, 2)
            stacks_out(0, 0)
            split_out(1)
            project_out(0, 3)
            stacks_out(0, 1)
            for t in range(2, BT):
                split_out(t)
                stacks_out(0, t)
            wkv_low(1)

            STATS = [{2: 1, 7: 2}, {0: 1, 1: 1, 2: 1, 7: 2}, {0: 1, 1: 1, 2: 2}]
            others, seen = slice(BT, TILES), [BT]

            def behind(k, s):
                if k == 0 and s < 2:
                    wkv_low(2 + s)
                if k == 0 and s == 2:
                    dve.wait_ge(x_rest, 16)
                for _ in range(STATS[k].get(s, 0)):
                    stat(seen[0])
                    seen[0] += 1
                if k == 2 and s == 3:
                    ask_deviations(others)
                if k == 2 and s == 7:
                    deviations(others)

            for k in range(3):
                unit(k, 0, first=(k == 0), between=lambda s: behind(k, s))
            assert seen[0] == TILES

            def turn(r):
                unit(3, r - 1)
                for k in range(3):
                    unit(k, r, ln2=r - 1)
            loop_over_batches(dve, tallies, turn)
            unit(3, BATCH - 1, last=True)
            finalize(BATCH - 1, GROUPS - 1, 1)

        att.close()

        TS = 2 * P
        NS = TOKENS // TS
        NA = 5
        NB = NS - NA
        MOST = 2 * TOKENS // TS + ER
        COLS = 2 * (MOST + NB)
        PART = (2 * TILES + 2 * NB) // 2
        RUNS = [(0, PART), (PART, 2 * TILES), (2 * TILES + 2 * NA, 3 * TILES)]
        FP16, INT32 = mybir.dt.float16, mybir.dt.int32

        w_sb = sb("w_sb", [P, 2, 2, 3, DC, D], FP32R)
        b_ug = sb("b_ug", [P, 2, 2, DC])
        bd = sb("bd", [P, 2, D])
        xg = sb("xg", [P, 2, D])
        x_hi, x_lo = sb("x_hi", [P, DC, TS], FP32R), sb("x_lo", [P, DC, TS], FP32R)
        u_hi, u_lo = sb("u_hi", [P, DC, TS], FP32R), sb("u_lo", [P, DC, TS], FP32R)
        s_sb, g_sb = sb("s_sb", [P, DC, TS]), sb("g_sb", [P, DC, TS])
        g_hi, g_lo = sb("g_hi", [P, DC, TS], FP32R), sb("g_lo", [P, DC, TS], FP32R)
        y_sb = sb("y_sb", [P, 2, D])
        whole = [P, TILES, ER]
        biased, key = sb("biased", whole), sb("key", whole)
        picked = sb("picked", [P, TILES + 1, ER])
        hot = sb("hot", [P, 2, TILES, ER])
        order, top = sb("order", [P, ER]), sb("top", [P, TILES])
        prob = sb("prob", [P, 2, TILES])
        before = sb("before", [P, P])
        ones = sb("ones", [P, P])
        prefix = sb("prefix", [P, TILES + 1, ER])
        tiles_i, tiles_f = sb("tiles_i", [P, ER], INT32), sb("tiles_f", [P, ER])
        start_f, start_i = sb("start_f", [P, ER + 1]), sb("start_i", [P, ER + 1], INT32)
        pos_f, pos_i = sb("pos_f", [P, 3, TILES]), sb("pos_i", [P, 3, TILES], INT32)
        col_i, col_f = sb("col_i", [P, 3, TILES], INT32), sb("col_f", [P, 3, TILES])
        row_f = sb("row_f", [P, 3, TILES])
        iota_f = sb("iota_f", [P, P])
        token = sb("token", [P, 3, TILES])
        hot_row, hot_col = sb("hot_row", [P, 2 * PART, P], FP16), sb("hot_col", [P, PART, COLS], FP16)
        iota_i = hot_row[:, 0:2, :].rearrange("p a n -> p (a n)").bitcast(INT32)
        token_i = hot_row[:, 2, :].bitcast(INT32)[:, 0:3 * TILES].rearrange("p (k t) -> p k t", t=TILES)
        table_f, table = sb("table_f", [P, COLS]), sb("table", [P, COLS], INT32)
        index = sb("index", [P, 2], INT32)
        yg = w_raw[:].rearrange("p m c n -> p (m c) n")
        RING = 3 * DC

        def two_banks(name):
            return ctx.enter_context(nc.psum_tensor(name, [P, 2, 2, TS], FP32))
        xt_ps, u_ps, z_ps, y_ps = two_banks("xt_ps"), two_banks("u_ps"), two_banks("z_ps"), two_banks("y_ps")
        y_v = y_ps[:].rearrange("p j a n -> p j (a n)")

        b_loaded = [sem("b_loaded0"), sem("b_loaded1")]
        var_ready, rstd_ready, gates_read = sem("var_ready"), sem("rstd_ready"), sem("gates_read")
        t2_ready, t2_done, gate_part, sel_ready, exp_ready = (
            sem(n) for n in ("t2_ready", "t2_done", "gate_part", "sel_ready", "exp_ready"))
        iota_set, before_set, picked_ready, window_ready, window_read = (
            sem(n) for n in ("iota_set", "before_set", "picked_ready", "window_ready", "window_read"))
        start_ready, hots_ready, table_ready, index_ready = (
            sem(n) for n in ("start_ready", "hots_ready", "table_ready", "index_ready"))
        xg_first = sem("xg_first")
        xg_loaded, xt_ready, xh_done, xl_done = (sem(n) for n in ("xg_loaded", "xt_ready", "xh_done", "xl_done"))
        u_ready, uh_done, ul_done, z_ready, s_done = (
            sem(n) for n in ("u_ready", "uh_done", "ul_done", "z_ready", "s_done"))
        g_done, gh_done, gl_done, y_ready, y_done = (
            sem(n) for n in ("g_done", "gh_done", "gl_done", "y_ready", "y_done"))
        y_stored, hi_done, lo_done = (
            sem(n) for n in ("y_stored", "hi_done", "lo_done"))
        yg_loaded = [sem(f"yg_loaded{i}") for i in range(RING)]
        added, out_stored, dve2 = sem("added"), sem("out_stored"), sem("dve2")
        block2 = ctx.enter_context(nc.Block())

        def routed(engine, head, tile, first_tile=None):
            engine.wait_ge(start_ready, 1)

            def start_of(e):
                at = start_i[0:1, e:e + 1] if isinstance(e, int) else start_i[0:1, bass.ds(e, 1)]
                return engine.value_load(at, min_val=0, max_val=MOST)

            def expert(j, par, nth, first, end):
                head(j, par, nth, first + NA)
                if first_tile is not None:
                    first_tile(j, first + NA, par)
                    first = first + 1
                with engine.Fori(first, end) as i:
                    tile(i + NA, par)

            with engine.Fori(0, ER // 2) as pair:
                s0, s1, s2 = start_of(pair * 2), start_of(pair * 2 + 1), start_of(pair * 2 + 2)
                expert(pair * 2 + 1, 1, pair, s0, s1)
                expert(pair * 2 + 2, 0, pair + 1, s1, s2)
            s0, s1 = start_of(ER - 1), start_of(ER)
            expert(ER, 1, ER // 2, s0, s1)
            return s1

        @block2.sync
        def _(sp):
            def load_weights(j):
                for m in range(3):
                    sp.dma_start(w_raw[:, m], w_all[bass.ds(j, 1), :, m].rearrange("a p c n -> p (a c) n"))\
                      .then_inc(raw_loaded[m], 16)

            def load_biases(j, par):
                sp.dma_start(b_ug[:, par], b_up_gate[bass.ds(j, 1)].rearrange("a p m c -> p (a m) c"))\
                  .then_inc(b_loaded[par], 16)
                sp.dma_start(bd[:, par, :], b_down[bass.ds(j, 1), :].to_broadcast([P, D])).then_inc(b_loaded[par], 16)

            for h in range(2):
                sp.dma_start(xg[:, h, :], xn_dram.rearrange("(t p) d -> p t d", p=P)[:, h, :]).then_inc(xg_first, 16)
            load_biases(0, 0)
            load_biases(1, 1)
            for t in range(TILES - BT, TILES):
                sp.wait_ge(n2_ready, t + 1)
                sp.dma_start(xn_dram.rearrange("(t p) d -> p t d", p=P)[:, t, :], y_sb[:, t % 2, :])\
                  .then_inc(n2_stored[t % 2], 16)
            sp.wait_ge(lo_done, 3)
            load_weights(1)
            sp.wait_ge(lo_done, 6)
            load_weights(2)

            def head(j, par, nth, first):
                sp.wait_ge(y_done, first * 2)
                load_biases(j + 1, 1 - par)
                if not isinstance(j, int):
                    sp.wait_ge(lo_done, j * 3 + 6)
                    load_weights(j + 2)

            def tile(n, par):
                for h in range(2):
                    sp.wait_ge(y_done, n * 2 + h + 1)
                    sp.dma_start(y_dram.rearrange("(s p) d -> p s d", p=P)[:, bass.ds((n - NA) * 2 + h, 1), :],
                                 y_sb[:, h:h + 1, :]).then_inc(y_stored, 16)
            routed(sp, head, tile)
            for t in range(TILES):
                sp.wait_ge(added, 2 * t + 2 if t < TILES - 2 else 2 * TILES + (t - (TILES - 3)))
                sp.dma_start(out.rearrange("(t p) d -> p t d", p=P)[:, t, :], x_sb[:, t, :]).then_inc(out_stored, 16)
            sp.wait_ge(out_stored, 16 * TILES)

        @block2.gpsimd
        def _(pool):
            def rows(n):
                pool.wait_ge(xt_ready, 2 * n)
                for h in range(2):
                    pool.dma_start(xg[:, h, :], xn_dram.rearrange("(t p) d -> p t d", p=P)[:, 2 * n + h, :])\
                        .then_inc(xg_loaded, 16)

            def gather(n):
                pool.wait_ge(xt_ready, n * 2)
                pool.wait_ge(table_ready, 1)
                nc.gpsimd.tensor_copy(index[:], table[:, bass.ds((n - NA) * 2, 2)]).then_inc(index_ready, 1)
                pool.wait_ge(index_ready, n - NA + 1)
                pool.sem_inc(passed)
                for h in range(2):
                    nc.gpsimd.indirect_dma_start(
                        out=xg[:, h, :], out_offset=None, in_=xn_dram,
                        in_offset=bass.IndirectOffsetOnAxis(ap=index[:, h:h + 1].bitcast(mybir.dt.uint32), axis=0),
                        ).then_inc(xg_loaded, 16)

            pool.wait_ge(var_ready, 1)
            nc.gpsimd.tensor_tensor(rsqrt[:, 0, 0:BT], mean_sq[:, 0, 0:BT], power[:, 0:BT], ALU.pow).then_inc(rstd_ready, 1)
            nc.gpsimd.iota(iota_i, [[1, P]], base=0, channel_multiplier=0).then_inc(iota_set, 1)
            nc.gpsimd.iota(token_i, [[0, 3], [P, TILES]], base=0, channel_multiplier=1).then_inc(iota_set, 1)
            nc.gpsimd.memset(ones[:], 1.0).then_inc(before_set, 1)
            pool.wait_ge(before_set, 1)
            nc.gpsimd.affine_select(out=before[:], in_=ones[:], compare_op=ALU.is_gt, fill=0.0, base=0,
                                    pattern=[[1, P]], channel_multiplier=-1).then_inc(before_set, 1)
            for n in range(1, NA):
                rows(n)
            for par in range(2):
                pool.wait_ge(n2_stored[par], 16 * TILES // 2)
            gather(NA)

            total = routed(pool, lambda j, par, nth, first: None, lambda n, par: gather(n + 1))

            def result(m):
                if m >= RING:
                    pool.wait_ge(added, m - RING + 1)
                nc.gpsimd.indirect_dma_start(
                    out=yg[:, m % RING, :], out_offset=None, in_=y_dram,
                    in_offset=bass.IndirectOffsetOnAxis(
                        ap=pos_i[:, m % 2, m // 2:m // 2 + 1].bitcast(mybir.dt.uint32), axis=0),
                    ).then_inc(yg_loaded[m % RING], 16)

            gather(total + NA + 1)
            pool.wait_ge(y_stored, total * 32)
            pool.sem_inc(passed)
            pool.wait_ge(lo_done, 3 * (ER + 2))
            for m in range(10):
                result(m)
            gather(total + NA + 2)
            for m in range(10, 2 * TILES):
                result(m)

        @block2.tensor
        def _(pe):
            def norm_transposes(t):
                pe.wait_ge(n2_ready, TILES - BT + t + 1)
                if t >= 2:
                    pe.wait_ge(t2_done, t - 1)
                else:
                    pe.wait_ge(xl_done, t + 1)
                bank = xt_ps[:, t % 2].rearrange("p a n -> p (a n)")
                for c in range(DC):
                    last = nc.tensor.transpose(bank[:, c * P:(c + 1) * P], y_sb[:, t % 2, c * P:(c + 1) * P], ident[:])
                last.then_inc(t2_ready, 1)

            def gates(t):
                pe.wait_ge(t2_done, t + 1)
                place = (s_sb, g_sb)[t % 2]
                at = z_ps[:, 0].rearrange("p a n -> p (a n)")[:, t * ER:(t + 1) * ER]
                for c in range(DC):
                    last = nc.tensor.matmul(at, place[:, c, 0:P], wr[:, c, :], start=(c == 0), stop=(c == DC - 1))
                last.then_inc(gate_part, 1)

            def three(out_ps, stat, mov, first, last):
                for a, b in ((0, 0), (0, 1), (1, 0)):
                    ins = nc.tensor.matmul(out_ps, stat[a], mov[b], start=(first and a + b == 0),
                                           stop=(last and a == 1), skip_group_check=True)
                return ins

            def x_transposes(n):
                if isinstance(n, int) and n == 0:
                    pe.wait_ge(xg_first, 32)
                else:
                    pe.wait_ge(xg_loaded, n * 32)
                for b in range(2):
                    for a in range(2):
                        c = 2 * b + a
                        for h in range(2):
                            last = nc.tensor.transpose(xt_ps[:, b, a, h * P:(h + 1) * P],
                                                       xg[:, h, c * P:(c + 1) * P], ident[:])
                    last.then_inc(xt_ready, 1)

            def prefixes():
                pe.wait_ge(picked_ready, 1)
                pe.wait_ge(before_set, 2)
                at = xt_ps[:, 0].rearrange("p a n -> p (a n)")[:, 0:(TILES + 1) * ER]\
                                .rearrange("p (t e) -> p t e", e=ER)
                nc.tensor.matmul(at, before[:], picked[:], start=True, stop=False, skip_group_check=True)
                for t in range(TILES):
                    behind = [P, TILES - t, ER]
                    last = nc.tensor.matmul(at[:, t + 1:, :], ones[:], picked[:, t:t + 1, :].to_broadcast(behind),
                                            start=False, stop=(t == TILES - 1), skip_group_check=True)
                last.then_inc(window_ready, 1)
                pe.wait_ge(window_read, 1)

            def table_part(w):
                pe.wait_ge(hots_ready, w + 1)
                at = xt_ps[:, 0].rearrange("p a n -> p (a n)")[:, 0:COLS]
                for i in range(PART):
                    last = nc.tensor.matmul(at, hot_row[:, w * PART + i, :], hot_col[:, i, :],
                                            start=(i == 0), stop=(i == PART - 1))
                last.then_inc(window_ready, 1)
                if w == 0:
                    pe.wait_ge(window_read, w + 2)

            def tile(n, par, ahead=None, behind_up=None, late_x=False, more=True):
                w = w_sb[:, par]
                known = isinstance(n, int)
                pe.wait_ge(xl_done, n * 2 + 2)
                if ahead:
                    ahead()
                for b in range(2):
                    if not known or n:
                        pe.wait_ge(g_done, n * 4 + (2 * b - 2))
                    if known and n == 0 and b == 0:
                        pe.wait_ge(lo_done, 1)
                    for c in range(DC):
                        for a in range(2):
                            cols = slice((2 * b + a) * P, (2 * b + a + 1) * P)
                            last = three(u_ps[:, b, a, :], (w[:, 0, 0, c, cols], w[:, 1, 0, c, cols]),
                                         (x_hi[:, c, :], x_lo[:, c, :]), c == 0 and a == 0, c == DC - 1)
                    last.then_inc(u_ready, 1)
                if behind_up:
                    behind_up()
                if more and not late_x:
                    x_transposes(n + 1)
                if known and n == 0:
                    pe.wait_ge(lo_done, 2)
                for b in range(2):
                    if not known or n:
                        pe.wait_ge(s_done, n * 4 + (2 * b - 2))
                    else:
                        pe.wait_ge(gates_read, 1)
                    for c in range(DC):
                        if b == 0:
                            pe.wait_ge(ul_done, n * 4 + (c + 1))
                        for a in range(2):
                            cols = slice((2 * b + a) * P, (2 * b + a + 1) * P)
                            last = three(z_ps[:, b, a, :], (w[:, 0, 1, c, cols], w[:, 1, 1, c, cols]),
                                         (u_hi[:, c, :], u_lo[:, c, :]), c == 0 and a == 0, c == DC - 1)
                    last.then_inc(z_ready, 1)
                if late_x:
                    pe.wait_ge(window_read, 3)
                    x_transposes(n + 1)
                if not known or n:
                    pe.wait_ge(y_done, n * 2)
                else:
                    pe.wait_ge(lo_done, 3)
                for c in range(DC):
                    pe.wait_ge(gl_done, n * 4 + (c + 1))
                    for h in range(2):
                        rows = slice(h * P, (h + 1) * P)
                        last = three(y_v[:, h, :], (g_hi[:, c, rows], g_lo[:, c, rows]),
                                     (w[:, 0, 2, c, :], w[:, 1, 2, c, :]), c == 0, c == DC - 1)
                        if c == DC - 1:
                            last.then_inc(y_ready, 1)

            def last_gates():
                for t in range(BT):
                    norm_transposes(t)
                    if t:
                        gates(t - 1)
                gates(BT - 1)

            x_transposes(0)
            tile(0, 0, behind_up=last_gates)
            tile(1, 0, behind_up=prefixes)
            tile(2, 0)
            tile(3, 0, behind_up=lambda: table_part(0))
            tile(4, 0, ahead=lambda: table_part(1), late_x=True)

            def head(j, par, nth, first):
                pe.wait_ge(lo_done, j * 3 + 3)
                pe.sem_inc(passed)
            total = routed(pe, head, tile)
            pe.wait_ge(lo_done, 3 * (ER + 2))
            for jj in range(NB):
                tile(total + (NA + jj), 0, more=jj < NB - 1)

        @block2.scalar
        def _(act):
            def split(j, par, m):
                act.wait_ge(raw_loaded[m], j * 16 + 16)
                nc.scalar.activation(w_sb[:, par, 0, m], w_raw[:, m], ACT.Copy).then_inc(hi_done, 1)

            def x_high(n):
                for b in range(2):
                    act.wait_ge(xt_ready, n * 2 + (b + 1))
                    nc.scalar.activation(x_hi[:, 2 * b:2 * b + 2, :], xt_ps[:, b], ACT.Copy).then_inc(xh_done, 1)

            def tile(n, par, more=True, during_z=None, during_y=None, late_x=False):
                for b in range(2):
                    act.wait_ge(u_ready, n * 2 + (b + 1))
                    for a in range(2):
                        c = 2 * b + a
                        last = nc.scalar.activation(u_hi[:, c, :], u_ps[:, b, a, :], ACT.Identity,
                                                    bias=b_ug[:, par, 0, c:c + 1])
                    last.then_inc(uh_done, 1)
                if more and not late_x:
                    x_high(n + 1)
                if during_z:
                    during_z()
                for b in range(2):
                    act.wait_ge(z_ready, n * 2 + (b + 1))
                    if not isinstance(n, int) or n:
                        act.wait_ge(g_done, n * 4)
                    for a in range(2):
                        c = 2 * b + a
                        nc.scalar.activation(s_sb[:, c, :], z_ps[:, b, a, :], ACT.Silu,
                                             bias=b_ug[:, par, 1, c:c + 1]).then_inc(s_done, 1)
                if late_x:
                    x_high(n + 1)
                if during_y:
                    during_y()

            def splits(j, par, ms):
                return lambda: [split(j, par, m) for m in ms]

            def choice_exp():
                act.wait_ge(sel_ready, 1)
                nc.scalar.activation(prob[:], prob[:], ACT.Exp).then_inc(exp_ready, 1)

            split(0, 0, 0)
            x_high(0)
            split(0, 0, 1)
            split(0, 0, 2)
            act.wait_ge(b_loaded[0], 32)
            tile(0, 0)
            tile(1, 0, during_z=choice_exp, during_y=splits(1, 1, [0]))
            tile(2, 0, during_y=splits(1, 1, [1, 2]))
            tile(3, 0)
            tile(4, 0, late_x=True)

            def head(j, par, nth, first):
                act.wait_ge(b_loaded[par], nth * 32 + 32)

            def first_tile(j, n, par):
                def one():
                    act.wait_ge(y_ready, n * 2)
                    split(j + 1, 1 - par, 0)
                tile(n, par, during_z=one, during_y=splits(j + 1, 1 - par, [1, 2]))
            total = routed(act, head, tile, first_tile)
            act.wait_ge(b_loaded[0], 32 * (ER // 2 + 2))
            for jj in range(NB):
                tile(total + (NA + jj), 0, more=jj < NB - 1)

        @block2.vector
        def _(dve):
            steps = [0]

            def done(ins):
                steps[0] += 1
                ins.then_inc(dve2, 1)
                dve.wait_ge(dve2, steps[0])

            def split(j, par, m):
                dve.wait_ge(hi_done, j * 3 + (m + 1))
                nc.vector.tensor_tensor(w_sb[:, par, 1, m], w_raw[:, m], w_sb[:, par, 0, m].bitcast(FP32),
                                        ALU.subtract).then_inc(lo_done, 1)

            def splits(j, par, ms):
                return lambda: [split(j, par, m) for m in ms]

            def x_low(n):
                for b in range(2):
                    dve.wait_ge(xh_done, n * 2 + (b + 1))
                    two = slice(2 * b, 2 * b + 2)
                    nc.vector.tensor_tensor(x_lo[:, two, :], xt_ps[:, b], x_hi[:, two, :].bitcast(FP32), ALU.subtract)\
                      .then_inc(xl_done, 1)

            last_batch = TILES - BT
            for t in range(BT):
                done(nc.vector.bn_stats(stats[:], x_sb[:, last_batch + t, :]))
                done(nc.vector.bn_aggr(mv2[:, t, :], stats[:]))
            nc.vector.tensor_scalar(mean_sq[:, 0, 0:BT], mv2[:, :, 1], LN_EPS, None, ALU.add).then_inc(var_ready, 1)
            split(0, 0, 0)
            x_low(0)
            dve.wait_ge(rstd_ready, 1)

            def norm(t):
                nc.vector.tensor_scalar(y_sb[:, t % 2, :], x_sb[:, last_batch + t, :], mv2[:, t, 0:1],
                                        rsqrt[:, 0, t:t + 1], ALU.subtract, ALU.mult).then_inc(n2_ready, 1)

            norm(0)
            norm(1)
            split(0, 0, 1)

            def last_gates():
                for t in range(BT):
                    dve.wait_ge(t2_ready, t + 1)
                    if t >= 2:
                        dve.wait_ge(gate_part, t - 1)
                    place = (s_sb, g_sb)[t % 2]
                    nc.vector.tensor_copy(place[:, :, 0:P], xt_ps[:, t % 2].rearrange("p a (h n) -> p (a h) n", n=P))\
                      .then_inc(t2_done, 1)
                    if t + 2 < BT:
                        dve.wait_ge(n2_stored[t % 2], 16 * (TILES // 2 - 1))
                        norm(t + 2)
                dve.wait_ge(gate_part, BT)
                gates = z_ps[:, 0].rearrange("p a n -> p (a n)")[:, 0:BT * ER].rearrange("p (t e) -> p t e", e=ER)
                nc.vector.tensor_tensor(gate[:, last_batch:, :], gates, brt[:].unsqueeze(1)
                                        .to_broadcast([P, BT, ER]), ALU.add).then_inc(gates_read, 1)

            def begin_choice():
                for e in range(ER):
                    nc.vector.memset(order[:, e:e + 1], float(ER - e))
                dve.wait_ge(iota_set, 2)
                done(nc.vector.tensor_copy(iota_f[:], iota_i))
                done(nc.vector.tensor_copy(token[:], token_i))
                nc.vector.memset(picked[:, TILES:, :], 0.0)
                dve.wait_ge(gates_read, 1)
                done(nc.vector.tensor_tensor(biased[:], gate[:], gbt[:].unsqueeze(1).to_broadcast(whole), ALU.add))

            def choose(k):
                done(nc.vector.tensor_reduce(top[:], biased[:], axis=AX.X, op=ALU.max))
                done(nc.vector.tensor_tensor(key[:], biased[:], top[:].unsqueeze(2).to_broadcast(whole), ALU.is_equal))
                done(nc.vector.tensor_tensor(key[:], key[:], order[:].unsqueeze(1).to_broadcast(whole), ALU.mult))
                done(nc.vector.tensor_reduce(top[:], key[:], axis=AX.X, op=ALU.max))
                done(nc.vector.tensor_tensor(hot[:, k], key[:], top[:].unsqueeze(2).to_broadcast(whole), ALU.is_equal))
                done(nc.vector.tensor_tensor(key[:], hot[:, k], gate[:], ALU.mult))
                done(nc.vector.tensor_reduce(prob[:, k, :], key[:], axis=AX.X, op=ALU.add))
                if k == 0:
                    done(nc.vector.scalar_tensor_tensor(biased[:], hot[:, 0], -3e38, biased[:], ALU.mult, ALU.add))

            both = [P, 2, TILES]

            def chosen():
                nc.vector.tensor_tensor(picked[:, 0:TILES, :], hot[:, 0], hot[:, 1], ALU.add).then_inc(picked_ready, 1)
                done(nc.vector.tensor_tensor(top[:], prob[:, 0, :], prob[:, 1, :], ALU.max))
                nc.vector.tensor_tensor(prob[:], prob[:], top[:].unsqueeze(1).to_broadcast(both), ALU.subtract)\
                  .then_inc(sel_ready, 1)

            def probabilities():
                dve.wait_ge(exp_ready, 1)
                done(nc.vector.tensor_tensor(top[:], prob[:, 0, :], prob[:, 1, :], ALU.add))
                done(nc.vector.reciprocal(top[:], top[:]))
                done(nc.vector.tensor_tensor(prob[:], prob[:], top[:].unsqueeze(1).to_broadcast(both), ALU.mult))

            def prefixes_out():
                dve.wait_ge(window_ready, 1)
                nc.vector.tensor_copy(prefix[:], xt_ps[:, 0].rearrange("p a n -> p (a n)")[:, 0:(TILES + 1) * ER]
                                      .rearrange("p (t e) -> p t e", e=ER)).then_inc(window_read, 1)

            def starts():
                dve.wait_ge(window_read, 1)
                done(nc.vector.tensor_scalar(tiles_i[:], prefix[:, TILES, :], float(TS - 1), None, ALU.add))
                done(nc.vector.tensor_scalar(tiles_i[:], tiles_i[:], 8, None, ALU.arith_shift_right))
                done(nc.vector.tensor_scalar(tiles_f[:], tiles_i[:], 1.0, None, ALU.max))
                done(nc.vector.memset(start_f[:, 0:1], 0.0))
                for e in range(ER):
                    done(nc.vector.tensor_tensor(start_f[:, e + 1:e + 2], start_f[:, e:e + 1], tiles_f[:, e:e + 1],
                                                 ALU.add))
                nc.vector.tensor_copy(start_i[:], start_f[:]).then_inc(start_ready, 1)

            def positions():
                slots = prefix[:, 0:TILES, :]
                done(nc.vector.scalar_tensor_tensor(slots, start_f[:, 0:ER].unsqueeze(1).to_broadcast(whole),
                                                    float(TS), slots, ALU.mult, ALU.add))
                for k in range(2):
                    done(nc.vector.tensor_tensor(key[:], hot[:, k], slots, ALU.mult))
                    done(nc.vector.tensor_reduce(pos_f[:, k, :], key[:], axis=AX.X, op=ALU.add))
                done(nc.vector.tensor_scalar(top[:, 0:1], start_f[:, ER:], float(TS), float(-TS * NA), ALU.mult, ALU.add))
                done(nc.vector.tensor_scalar(pos_f[:, 2, :], token[:, 2, :], top[:, 0:1], None, ALU.add))
                done(nc.vector.tensor_copy(pos_i[:], pos_f[:]))
                done(nc.vector.tensor_scalar(col_i[:], pos_i[:], 7, None, ALU.arith_shift_right))
                done(nc.vector.tensor_copy(col_f[:], col_i[:]))
                done(nc.vector.scalar_tensor_tensor(row_f[:], col_f[:], float(-P), pos_f[:], ALU.mult, ALU.add))

            def run_of(i):
                begin, end = RUNS[i]
                at = begin if i < 2 else 2 * TILES
                return slice(begin, end), slice(at, at + end - begin), end - begin

            def hot_rows(i):
                pairs, at, n = run_of(i)
                place = row_f[:].rearrange("p k t -> p (k t)")[:, pairs]
                nc.vector.tensor_tensor(hot_row[:, at, :], iota_f[:].unsqueeze(1).to_broadcast([P, n, P]),
                                        place.unsqueeze(2).to_broadcast([P, n, P]), ALU.is_equal)

            def hot_cols(i):
                pairs, at, n = run_of(i)
                if i:
                    at = slice(at.start - PART, at.stop - PART)
                wide = [P, n, COLS]
                place = col_f[:].rearrange("p k t -> p (k t)")[:, pairs]
                number = token[:].rearrange("p k t -> p (k t)")[:, pairs]
                done(nc.vector.tensor_tensor(hot_col[:, at, :], iota_f[:, 0:COLS].unsqueeze(1).to_broadcast(wide),
                                             place.unsqueeze(2).to_broadcast(wide), ALU.is_equal))
                last = nc.vector.tensor_tensor(hot_col[:, at, :], hot_col[:, at, :],
                                               number.unsqueeze(2).to_broadcast(wide), ALU.mult)
                if i != 1:
                    last.then_inc(hots_ready, 1)

            def table_out(w):
                dve.wait_ge(window_ready, w + 2)
                part = xt_ps[:, 0].rearrange("p a n -> p (a n)")[:, 0:COLS]
                if w == 0:
                    nc.vector.tensor_copy(table_f[:], part).then_inc(window_read, 1)
                else:
                    nc.vector.tensor_tensor(table[:], table_f[:], part, ALU.add).then_inc(window_read, 1)
                    dve.wait_ge(window_read, w + 2)
                    nc.vector.memset(top[:, 0:1], 0.0).then_inc(table_ready, 1)

            def tile(n, par, more=True, x_tile=None, before_x=None, during_z=None, during_y=None, late_x=False,
                     last=False):
                bias = b_ug[:, par, 0]
                for b in range(2):
                    dve.wait_ge(uh_done, n * 2 + (b + 1))
                    for a in range(2):
                        c = 2 * b + a
                        nc.vector.scalar_tensor_tensor(u_lo[:, c, :], u_ps[:, b, a, :], bias[:, c:c + 1],
                                                       u_hi[:, c, :].bitcast(FP32), ALU.add, ALU.subtract)\
                          .then_inc(ul_done, 1)
                if before_x:
                    before_x()
                if more and not late_x:
                    x_low(n + 1)
                if during_z:
                    during_z()
                for c in range(DC):
                    b, a = divmod(c, 2)
                    dve.wait_ge(s_done, n * 4 + (c + 1))
                    nc.vector.scalar_tensor_tensor(g_sb[:, c, :], u_ps[:, b, a, :], bias[:, c:c + 1],
                                                   s_sb[:, c, :], ALU.add, ALU.mult).then_inc(g_done, 1)
                    dve.wait_ge(g_done, n * 4 + (c + 1))
                    nc.vector.tensor_copy(g_hi[:, c, :], g_sb[:, c, :]).then_inc(gh_done, 1)
                    dve.wait_ge(gh_done, n * 4 + (c + 1))
                    nc.vector.tensor_tensor(g_lo[:, c, :], g_sb[:, c, :], g_hi[:, c, :].bitcast(FP32),
                                            ALU.subtract).then_inc(gl_done, 1)
                if late_x:
                    x_low(n + 1)
                if during_y:
                    during_y()
                for h in range(2):
                    dve.wait_ge(y_ready, n * 2 + (h + 1))
                    if x_tile is None and h == 0:
                        dve.wait_ge(y_stored, (n - NA) * 32)
                    nc.vector.tensor_tensor(y_sb[:, h, :], y_v[:, h, :], bd[:, par, :], ALU.add).then_inc(y_done, 1)
                    if x_tile is not None:
                        dve.wait_ge(y_done, n * 2 + (h + 1))
                        at = x_sb[:, x_tile + h, :]
                        ins = nc.vector.tensor_tensor(at, at, y_sb[:, h, :], ALU.add)
                        if last:
                            ins.then_inc(added, 1)

            def steps_of(*parts):
                return lambda: [part() for part in parts]

            dve.wait_ge(b_loaded[0], 32)
            def stored():
                for par in range(2):
                    dve.wait_ge(n2_stored[par], 16 * TILES // 2)

            tile(0, 0, x_tile=0, before_x=last_gates, during_z=steps_of(lambda: split(0, 0, 2), begin_choice),
                 during_y=steps_of(lambda: choose(0), lambda: choose(1), chosen, stored))
            tile(1, 0, x_tile=2, before_x=prefixes_out, during_z=probabilities, during_y=steps_of(starts, positions))
            tile(2, 0, x_tile=4, during_z=lambda: hot_rows(0), during_y=steps_of(lambda: hot_cols(0), lambda: hot_rows(1)))
            tile(3, 0, x_tile=6, before_x=lambda: table_out(0),
                 during_z=steps_of(lambda: hot_cols(1), lambda: hot_rows(2)),
                 during_y=steps_of(lambda: hot_cols(2), splits(1, 1, [0])))
            table_out(1)
            tile(4, 0, x_tile=8, during_z=splits(1, 1, [1]), during_y=splits(1, 1, [2]), late_x=True)

            def head(j, par, nth, first):
                dve.wait_ge(b_loaded[par], nth * 32 + 32)
                dve.sem_inc(passed)

            def first_tile(j, n, par):
                tile(n, par, during_y=splits(j + 1, 1 - par, range(3)))
            total = routed(dve, head, tile, first_tile)
            dve.wait_ge(b_loaded[0], 32 * (ER // 2 + 2))
            dve.wait_ge(y_stored, total * 32)

            def add(t):
                for k in range(2):
                    m = 2 * t + k
                    dve.wait_ge(yg_loaded[m % RING], 16 * (m // RING + 1))
                    if k:
                        dve.wait_ge(added, m)
                    nc.vector.scalar_tensor_tensor(x_sb[:, t, :], yg[:, m % RING, :], prob[:, k, t:t + 1], x_sb[:, t, :],
                                                   ALU.mult, ALU.add).then_inc(added, 1)

            def adds(*tiles):
                return lambda: [add(t) for t in tiles]

            tile(total + NA, 0, x_tile=2 * NA, during_z=adds(0), during_y=adds(1, 2, 3, 4))
            tile(total + (NA + 1), 0, x_tile=2 * (NA + 1), during_z=adds(5, 6), during_y=adds(7, 8, 9, 10))
            tile(total + (NA + 2), 0, more=False, x_tile=2 * (NA + 2), during_z=adds(11, 12),
                 during_y=adds(13, 14, 15), last=True)


def kernel(**inputs):
    import numpy as np
    import concourse.bacc as bacc
    from concourse.bass_utils import run_bass_kernel_spmd

    nc = bacc.Bacc("TRN2", target_bir_lowering=False, num_devices=1, dynamic_dma_scratch_size=8192)
    a = {k.replace("L0_", ""): np.asarray(v) for k, v in inputs.items()}
    x, context = a["x"], a["ctx_2048"]
    d = x.shape[-1]
    kv = np.concatenate([a["xattn_Wk"], a["xattn_Wv"]], axis=0)
    wk, wv = kv[0::2].T.reshape(d, -1, 1, P), kv[1::2].T.reshape(d, -1, 1, P)
    f = {n: a["ffn_" + n] for n in ("Wr", "br", "gate_bias", "Wup", "bup", "Wgate", "bgate", "Wdown", "bdown",
                                    "Wsu", "bsu", "Wsg", "bsg", "Wsd", "bsd")}
    w = np.stack([np.concatenate([f[s][None], f[r], f[s][None]]) for r, s in (
        ("Wup", "Wsu"), ("Wgate", "Wsg"), ("Wdown", "Wsd"))], axis=1)
    b = np.stack([np.concatenate([f[s][None], f[r], f[s][None]]) for r, s in (("bup", "bsu"), ("bgate", "bsg"))],
                 axis=1)
    arrays = {
        "x": x.reshape(-1, d),
        "ctx_t": context.transpose(0, 2, 1),
        "wq_t": a["xattn_Wq"].T,
        "wkv_t": np.concatenate([wk, wv], axis=2).reshape(d, -1),
        "w_all": w.reshape(w.shape[0], 3, d // P, P, d).transpose(0, 3, 1, 2, 4),
        "b_up_gate": b.reshape(b.shape[0], 2, d // P, P).transpose(0, 3, 1, 2),
        "b_down": np.concatenate([f["bsd"][None], f["bdown"], f["bsd"][None]]),
        "w_router": f["Wr"].reshape(d // P, P, -1).transpose(1, 0, 2),
        "b_router": f["br"],
        "gate_bias": f["gate_bias"],
    }
    arrays = {k: np.ascontiguousarray(v) for k, v in arrays.items()}
    args = [nc.dram_tensor(k, v.shape, mybir.dt.from_np(v.dtype), kind="ExternalInput").ap()
            for k, v in arrays.items()]
    n = arrays["x"].shape[0]
    args.append(nc.dram_tensor("xn_dram", (n, d), FP32, kind="Internal").ap())
    args.append(nc.dram_tensor("y_dram", (2 * n + 2 * P * f["Wr"].shape[1], d), FP32, kind="Internal").ap())
    out = nc.dram_tensor("out", arrays["x"].shape, FP32, kind="ExternalOutput").ap()
    moe_layer(nc, *args, out)
    r = run_bass_kernel_spmd(nc, [arrays], core_ids=[0])
    return r.results[0]["out"].reshape(x.shape)
```
